# Optimizing a Trainium2 kernel written in Bass

```python
import numpy as np
import jax
import jax.numpy as jnp

def _softmax(x, axis=-1):
    return jax.nn.softmax(x, axis=axis)
def _gelu(x):
    return jax.nn.gelu(x, approximate=True)
def _silu(x):
    return jax.nn.silu(x)
def _sigmoid(x):
    return jax.nn.sigmoid(x)
def _layernorm(x, axis=-1, eps=1e-5):
    m = jnp.mean(x, axis=axis, keepdims=True)
    v = jnp.var(x, axis=axis, keepdims=True)
    return (x - m) / jnp.sqrt(v + eps)
def _scatter_add(tgt, idx, src, axis=0):
    return tgt.at[idx].add(src)
def _segment_sum(src, seg, n):
    return jax.ops.segment_sum(src, seg, n)

kernel_name = 'mk_metaformer_d1_conv_nchw512_d042e2'

def setup_inputs(seed: int = 0):
    np.random.seed(seed)
    _w = jnp.asarray
    def _rec_inputs():
        import jax
        import jax.numpy as jnp
        _gk = jax.random.key(seed)
        x = -0.0002928 + 1 * jax.random.normal(jax.random.fold_in(_gk, 1), (8, 512, 32, 32), jnp.float32)
        return x
    x = _rec_inputs()
    def _L0_conv_setup():
        import jax, jax.numpy as jnp
        import numpy as np
        EMBED_DIM = 512
        NUM_HEADS = 8
        HEAD_DIM = EMBED_DIM // NUM_HEADS

        def _proj(x, W, b):
            return jnp.einsum('bchw,oc->bohw', x, W) + b[None, :, None, None]
        key = jax.random.key(seed)
        ks = jax.random.split(key, 9)
        C = EMBED_DIM
        s = 1.0 / np.sqrt(C)
        x = jax.random.normal(ks[0], (8, C, 32, 32), dtype=jnp.float32)
        return {'x': x, 'Wq': jax.random.normal(ks[1], (C, C), dtype=jnp.float32) * s, 'bq': jax.random.normal(ks[2], (C,), dtype=jnp.float32) * s, 'Wk': jax.random.normal(ks[3], (C, C), dtype=jnp.float32) * s, 'bk': jax.random.normal(ks[4], (C,), dtype=jnp.float32) * s, 'Wv': jax.random.normal(ks[5], (C, C), dtype=jnp.float32) * s, 'bv': jax.random.normal(ks[6], (C,), dtype=jnp.float32) * s, 'Wo': jax.random.normal(ks[7], (C, C), dtype=jnp.float32) * s, 'bo': jax.random.normal(ks[8], (C,), dtype=jnp.float32) * s}
    _L0_conv_all = _L0_conv_setup()
    _L0_conv_in = {k: v for k, v in _L0_conv_all.items() if k in ('Wq', 'bq', 'Wk', 'bk', 'Wv', 'bv', 'Wo', 'bo', )}
    del _L0_conv_all

    def _L0_ffn_setup():
        import jax, jax.numpy as jnp
        import numpy as np
        B, S, D = (8, 8192, 512)
        E, DFF = (16, 512)
        CAPACITY = 2
        key = jax.random.key(seed)
        ks = jax.random.split(key, 4)
        x = jax.random.normal(ks[0], (B, S, D), dtype=jnp.float32)
        gate_weight = jax.random.normal(ks[1], (D, E), dtype=jnp.float32) * 0.006
        w1 = jax.random.normal(ks[2], (E, D, DFF), dtype=jnp.float32) * 0.02
        b1 = jnp.zeros((E, DFF), dtype=jnp.float32)
        w2 = jax.random.normal(ks[3], (E, DFF, D), dtype=jnp.float32) * 0.02
        b2 = jnp.zeros((E, D), dtype=jnp.float32)
        return {'x': x, 'gate_weight': gate_weight, 'w1': w1, 'b1': b1, 'w2': w2, 'b2': b2}
    _L0_ffn_all = _L0_ffn_setup()
    _L0_ffn_in = {k: v for k, v in _L0_ffn_all.items() if k in ('gate_weight', 'w1', 'b1', 'w2', 'b2', )}
    del _L0_ffn_all

    return {
        "x": x,
        "L0_conv_Wq": _L0_conv_in["Wq"],
        "L0_conv_bq": _L0_conv_in["bq"],
        "L0_conv_Wk": _L0_conv_in["Wk"],
        "L0_conv_bk": _L0_conv_in["bk"],
        "L0_conv_Wv": _L0_conv_in["Wv"],
        "L0_conv_bv": _L0_conv_in["bv"],
        "L0_conv_Wo": _L0_conv_in["Wo"],
        "L0_conv_bo": _L0_conv_in["bo"],
        "L0_ffn_gate_weight": _L0_ffn_in["gate_weight"],
        "L0_ffn_w1": _L0_ffn_in["w1"],
        "L0_ffn_b1": _L0_ffn_in["b1"],
        "L0_ffn_w2": _L0_ffn_in["w2"],
        "L0_ffn_b2": _L0_ffn_in["b2"],
    }

def reference(x, L0_conv_Wq, L0_conv_bq, L0_conv_Wk, L0_conv_bk, L0_conv_Wv, L0_conv_bv, L0_conv_Wo, L0_conv_bo, L0_ffn_gate_weight, L0_ffn_w1, L0_ffn_b1, L0_ffn_w2, L0_ffn_b2):
    import jax
    import jax.numpy as jnp
    def _L0_conv_ref(x, Wq, bq, Wk, bk, Wv, bv, Wo, bo):
        import jax, jax.numpy as jnp
        import numpy as np
        EMBED_DIM = 512
        NUM_HEADS = 8
        HEAD_DIM = EMBED_DIM // NUM_HEADS

        def _proj(x, W, b):
            return jnp.einsum('bchw,oc->bohw', x, W) + b[None, :, None, None]
        B, C, H, W = x.shape
        h, d = (NUM_HEADS, HEAD_DIM)
        scale = d ** (-0.5)
        q = _proj(x, Wq, bq).reshape(B, h, d, H * W).transpose(0, 1, 3, 2)
        k = _proj(x, Wk, bk).reshape(B, h, d, H * W).transpose(0, 1, 3, 2)
        v = _proj(x, Wv, bv).reshape(B, h, d, H * W).transpose(0, 1, 3, 2)
        scores = jnp.einsum('bhnd,bhmd->bhnm', q, k) * scale
        attn = jax.nn.softmax(scores, axis=-1)
        out = jnp.einsum('bhnm,bhmd->bhnd', attn, v)
        out = out.transpose(0, 1, 3, 2).reshape(B, C, H, W)
        return _proj(out, Wo, bo)

    def _L0_ffn_ref(x, gate_weight, w1, b1, w2, b2):
        import jax, jax.numpy as jnp
        import numpy as np
        B, S, D = (8, 8192, 512)
        E, DFF = (16, 512)
        CAPACITY = 2
        Bx, Sx, Dx = x.shape
        num_experts = gate_weight.shape[1]
        k = Sx // num_experts * CAPACITY
        logits = jnp.einsum('bsd,de->bse', x, gate_weight)
        affinity = jax.nn.softmax(logits, axis=-1).transpose(0, 2, 1)
        gating, index = jax.lax.top_k(affinity, k)
        x_in = jnp.take_along_axis(x[:, None, :, :], index[..., None], axis=2)
        h = jax.nn.gelu(jnp.einsum('bekd,edh->bekh', x_in, w1) + b1[None, :, None, :])
        x_e = jnp.einsum('bekh,ehd->bekd', h, w2) + b2[None, :, None, :]
        weighted = gating[..., None] * x_e
        out = jnp.zeros_like(x)
        idx_flat = index.reshape(Bx, num_experts * k)
        vals_flat = weighted.reshape(Bx, num_experts * k, Dx)
        out = out.at[jnp.arange(Bx)[:, None], idx_flat].add(vals_flat)
        return out

    def _gn(v, G=32, eps=1e-5):
        B_, C_, H_, W_ = v.shape
        g = v.reshape(B_, G, C_ // G, H_, W_)
        m = jnp.mean(g, axis=(2, 3, 4), keepdims=True)
        s = jnp.var(g, axis=(2, 3, 4), keepdims=True)
        return ((g - m) / jnp.sqrt(s + eps)).reshape(v.shape)

    def _ln_c(v, eps=1e-6):
        m = jnp.mean(v, axis=1, keepdims=True)
        s = jnp.var(v, axis=1, keepdims=True)
        return (v - m) / jnp.sqrt(s + eps)

    def _ln_t(v, eps=1e-5):
        m = jnp.mean(v, axis=-1, keepdims=True)
        s = jnp.var(v, axis=-1, keepdims=True)
        return (v - m) / jnp.sqrt(s + eps)

    def _to_tokens(v):
        B_, C_, H_, W_ = v.shape
        return v.reshape(B_, C_, H_ * W_).transpose(0, 2, 1)
    def _from_tokens(t, like):
        B_, C_, H_, W_ = like.shape
        return t.transpose(0, 2, 1).reshape(B_, C_, H_, W_)

    x = x + _L0_conv_ref(_ln_c(x), L0_conv_Wq, L0_conv_bq, L0_conv_Wk, L0_conv_bk, L0_conv_Wv, L0_conv_bv, L0_conv_Wo, L0_conv_bo)
    t = _to_tokens(x)
    t = t + _L0_ffn_ref(_ln_t(t), L0_ffn_gate_weight, L0_ffn_w1, L0_ffn_b1, L0_ffn_w2, L0_ffn_b2)
    x = _from_tokens(t, x)
    return x


_drawn_inputs = setup_inputs


def setup_inputs(seed=0):
    import zlib

    import numpy as np

    out = dict(_drawn_inputs(seed))
    spreads = {'L0_ffn_b1': (0.0, 0.8), 'L0_ffn_b2': (0.0, 0.731)}
    factors = {'L0_conv_bq': 8.0,
     'L0_conv_bk': 8.0,
     'L0_ffn_gate_weight': 3.54,
     'L0_ffn_w1': 4.632,
     'L0_ffn_w2': 4.339}
    for name, (base, spread) in spreads.items():
        noise = np.random.default_rng([zlib.crc32(name.encode()), seed]).standard_normal(out[name].shape)
        drawn = base * np.exp(spread * noise) if base else spread * noise
        out[name] = jnp.asarray(drawn.astype(out[name].dtype))
    for name, factor in factors.items():
        out[name] = (out[name] * factor).astype(out[name].dtype)
    return out
```

```python
from contextlib import ExitStack

import concourse.bass as bass
from concourse import mybir

F32 = mybir.dt.float32
F32R = mybir.dt.float32r
U32 = mybir.dt.uint32
ACT = mybir.ActivationFunctionType
ALU = mybir.AluOpType
AX = mybir.AxisListType

P = 128
B, C, N = 8, 512, 1024
NT = N // P
KC = C // P
H, D = 8, 64
PAIRS = H // 2
E, FF = 16, 512
CAP = N // E * 2
EPS1, EPS2 = 1e-6, 1e-5

UP = 2 * NT
UNITS = PAIRS * UP
BLOCKS = UNITS // 2
QC = 2 * P

RING = NT + PAIRS * 4 + 2 * UNITS


def ring_norm(i):
    return i


def ring_proj(p, r):
    return NT + 4 * p + (2 * (UP * p - 1) if p else 0) + r


def ring_probs(u, c):
    return NT + 4 * min(PAIRS, (u + 1) // UP + 1) + 2 * u + c


def split_weights_dram(nc):
    wqk = nc.dram_tensor("wqk_split", [PAIRS, P, 4, KC, P], F32).ap()
    wvo = nc.dram_tensor("wvo_split", [2, P, 2, KC, C], F32).ap()
    return wqk, wvo


def attention(nc, x, wT, b_row, b_col, gate, out, n2_dram, aff_dram, ident):
    wqk_dram, wvo_dram = split_weights_dram(nc)
    with ExitStack() as ctx:
        def sb(name, shape, dt=F32):
            return ctx.enter_context(nc.sbuf_tensor(name, shape, dt))

        def sem(name):
            return ctx.enter_context(nc.semaphore(name))

        wqk = sb("wqk", [P, 2, 4, KC, P], F32R)
        wvo = sb("wvo", [P, 2, KC, C], F32R)
        xt = sb("xt", [P, NT, C])
        nT = sb("nT", [P, 2, KC, N], F32R)
        qk = sb("qk", [P, 2, 2, N], F32R)
        V = sb("V", [P, NT, PAIRS, 4, D], F32R)
        prob = sb("prob", [P, 2, N])
        tok = prob[:, :, :].rearrange("p a (s c) -> p (a s) c", c=C)
        PT = sb("PT", [P, 2, 2, NT, QC], F32R)
        oS = PT[:, :, :, :, :].rearrange("p h b t q -> p h (b t q)").rearrange(
            "p h (k n) -> p h k n", k=KC)
        oT = sb("oT", [P, KC, N])
        n2T = oT[:, :, :].rearrange("p k n -> p (k n)").rearrange("p (i k t) -> p i k t", i=NT, k=KC)
        affT = oT[0:E, 0, :]
        bv_bc = sb("bv_bc", [P, C])
        bo_bc = sb("bo_bc", [P, C])
        bqk = sb("bqk", [P, 2, KC])
        gate_sb = sb("gate_sb", [P, KC, E])
        nmax = sb("nmax", [P, UNITS])
        rsum = sb("rsum", [P, UNITS])
        rinv = sb("rinv", [P, UNITS])
        ones = sb("ones", [P, P])
        rinv_bc = sb("rinv_bc", [P, 2, 2, P])
        Rs = sb("Rs", [P, 2, QC])
        oL = sb("oL", [P, 2, QC])
        oSum = sb("oSum", [P, 2, QC])
        stats = sb("stats", [P, NT, 6])
        mv = sb("mv", [P, NT, 2])
        ve = sb("ve", [P, NT])
        std = sb("std", [P, NT])
        r0 = sb("r0", [P, NT])
        r1 = sb("r1", [P, NT])
        rstd = sb("rstd", [P, NT])
        lg = sb("lg", [P, NT, E])
        aff = sb("aff", [P, NT, E])
        gmax = sb("gmax", [P, NT])
        gsum = sb("gsum", [P, NT])
        grec = sb("grec", [P, NT])

        S = ctx.enter_context(nc.psum_tensor("S", [P, 2, N], F32))
        ring = ctx.enter_context(nc.psum_tensor("ring", [P, 2, 512], F32))
        O = ctx.enter_context(nc.psum_tensor("O", [P, 2, 512], F32))
        S4 = S[:, :, :].rearrange("p a (h n) -> p (a h) n", h=2)

        w_raw_in = sem("w_raw_in")
        w_hi = sem("w_hi")
        w_lo = sem("w_lo")
        w_out = sem("w_out")
        consts_in = sem("consts_in")
        bq_scaled = sem("bq_scaled")
        ones_set = sem("ones_set")
        x_in = [sem(f"x_in{i}") for i in range(2)]
        wv_in = sem("wv_in")
        wo_in = sem("wo_in")
        wqk_in = [sem(f"wqk_in{i}") for i in range(2)]
        t_out = sem("t_out")
        n2_out = [sem(f"n2_out{i}") for i in range(4)]
        aff_out = sem("aff_out")
        stats_done = sem("stats_done")
        mv_done = sem("mv_done")
        ve_done = sem("ve_done")
        std_done = sem("std_done")
        newton = sem("newton")
        norm_done = sem("norm_done")
        ring_filled = sem("ring_filled")
        ring_hi = sem("ring_hi")
        ring_lo = sem("ring_lo")
        o_filled = sem("o_filled")
        v_sum = sem("v_sum")
        v_hi = sem("v_hi")
        v_lo = sem("v_lo")
        xbo = sem("xbo")
        s_filled = sem("s_filled")
        max_done = sem("max_done")
        exp_done = sem("exp_done")
        rinv_done = sem("rinv_done")
        rbc_done = sem("rbc_done")
        pv_done = sem("pv_done")
        o_copied = sem("o_copied")
        o_sum = sem("o_sum")
        o_norm = sem("o_norm")
        os_hi = sem("os_hi")
        os_lo = sem("os_lo")
        t_done = sem("t_done")
        n2_filled = sem("n2_filled")
        n2_copied = sem("n2_copied")
        logits = sem("logits")
        soft = sem("soft")
        soft_exp = sem("soft_exp")
        affT_filled = sem("affT_filled")
        affT_copied = sem("affT_copied")
        sp_passed, pool_passed, dve_passed = sem("sp_passed"), sem("pool_passed"), sem("dve_passed")

        block = ctx.enter_context(nc.Block())

        @block.sync
        def _(sp):
            sp.dma_start(bv_bc[:, :], b_row[2:3, :].broadcast_to([P, C])).then_inc(consts_in, 16)
            sp.dma_start(bo_bc[:, :], b_row[3:4, :].broadcast_to([P, C])).then_inc(consts_in, 16)
            sp.dma_start(bqk[:, :, :], b_col).then_inc(consts_in, 16)
            sp.dma_start(gate_sb[:, :, :], gate).then_inc(consts_in, 16)
            for r in range(2):
                if r:
                    sp.wait_ge(w_lo, 2)
                for j in range(2):
                    sp.dma_start(xt[:, KC * j:KC * j + KC, :], wT[2 * r + j]).then_inc(w_raw_in, 16)
                for j in range(2):
                    sp.wait_ge(w_lo, 2 * r + j + 1)
                    for h in range(2):
                        half = oS[:, h, :, :].rearrange("p k n -> p (k n)").bitcast(F32).rearrange(
                            "p (w k c) -> p w k c", w=2, k=KC)[:, j, :, :]
                        if r == 0:
                            for p in range(PAIRS):
                                sp.dma_start(wqk_dram[p, :, 2 * j + h, :, :],
                                             half[:, :, p * P:(p + 1) * P]).then_inc(w_out, 16)
                        else:
                            sp.dma_start(wvo_dram[j, :, h, :, :], half).then_inc(w_out, 16)
                if r == 0:
                    sp.wait_ge(w_out, 16 * 4 * PAIRS)
            sp.wait_ge(w_out, 16 * (4 * PAIRS + 4))

            with sp.Fori(0, B) as b:
                def load_pair(p):
                    sp.dma_start(wqk[:, p % 2, :, :, :].bitcast(F32), wqk_dram[p]).then_inc(wqk_in[p % 2], 16)

                for i in range(2):
                    sp.dma_start(xt[:, 4 * i:4 * i + 4, :],
                                 x[b, :, :].rearrange("(i p) c -> p i c", p=P)[:, 4 * i:4 * i + 4, :]
                                 ).then_inc(x_in[i], 16)
                sp.dma_start(wvo[:, :, :, :].bitcast(F32), wvo_dram[0]).then_inc(wv_in, 16)
                load_pair(0)
                load_pair(1)
                sp.wait_ge(o_filled, b * (2 * NT) + NT)
                sp.dma_start(wvo[:, :, :, :].bitcast(F32), wvo_dram[1]).then_inc(wo_in, 16)
                for p in range(2, PAIRS):
                    sp.wait_ge(ring_filled, b * RING + ring_proj(p - 2, 3) + 1)
                    load_pair(p)
                rows = out[b, :, :].rearrange("(i p) c -> i p c", p=P)
                n2_rows = n2_dram[b, :, :].rearrange("(i p) c -> i p c", p=P)
                for i in range(NT):
                    sp.wait_ge(t_done, b * NT + i + 1)
                    sp.dma_start(rows[i, :, :], xt[:, i, :]).then_inc(t_out, 16)
                for i in range(NT):
                    sp.wait_ge(norm_done, b * (2 * NT) + NT + i + 1)
                    sp.dma_start(n2_rows[i, :, :], tok[:, i % 4, :]).then_inc(n2_out[i % 4], 16)
                sp.wait_ge(affT_copied, b * 2 + 2)
                sp.dma_start(aff_dram[b, :, :], affT).then_inc(aff_out, 16)
                sp.wait_ge(t_out, b * (16 * NT) + 16 * NT)
                for i in range(4):
                    sp.wait_ge(n2_out[i], b * (4 * NT) + 4 * NT)
                sp.wait_ge(aff_out, b * 16 + 16)
                sp.sem_inc(sp_passed, 1)

        @block.gpsimd
        def _(pool):
            nc.gpsimd.memset(ones[:, :], 1.0).then_inc(ones_set, 1)
            pool.wait_ge(ones_set, 1)
            pool.wait_ge(consts_in, 64)
            with pool.Fori(0, B) as b:
                for i in range(NT):
                    pool.wait_ge(v_hi, b * NT + i + 1)
                    src = tok[:, i % 4, :].rearrange("p (a h d) -> p a h d", a=PAIRS, h=2)
                    nc.gpsimd.tensor_tensor(V[:, i, :, 1:3, :], src,
                                            V[:, i, :, 0:4:3, :].bitcast(F32), ALU.subtract).then_inc(v_lo, 1)
                for i in range(NT):
                    if i == 0:
                        pool.wait_ge(norm_done, b * (2 * NT) + NT)
                    nc.gpsimd.tensor_tensor(xt[:, i, :], xt[:, i, :], bo_bc[:, :], ALU.add).then_inc(xbo, 1)
                for k in range(BLOCKS + 2):
                    if k < BLOCKS:
                        if k >= 3:
                            pool.wait_ge(o_norm, b * BLOCKS + k - 2)
                        pool.wait_ge(rinv_done, b * BLOCKS + k + 1)
                        if k >= 2:
                            pool.wait_ge(pv_done, b * BLOCKS + k - 1)
                        pool.sem_inc(pool_passed, 1)
                        for j in range(2):
                            last = nc.gpsimd.tensor_scalar(rinv_bc[:, k % 2, j, :], ones[:, :],
                                                           rinv[:, 2 * k + j:2 * k + j + 1], None, ALU.mult)
                        last.then_inc(rbc_done, 1)
                    if k >= 2:
                        m = k - 2
                        pair, odd, q = m // NT, m // (NT // 2) % 2, m % (NT // 2)
                        rows = slice(D * odd, D * odd + D)
                        if k < BLOCKS:
                            pool.wait_ge(rbc_done, b * BLOCKS + k + 1)
                        pool.wait_ge(o_sum, b * BLOCKS + m + 1)
                        nc.gpsimd.tensor_tensor(oT[rows, pair, q * QC:(q + 1) * QC], oSum[rows, m % 2, :],
                                                Rs[rows, m % 2, :], ALU.mult).then_inc(o_norm, 1)
                for i in range(NT):
                    cols = slice(i * P, (i + 1) * P)
                    if i == 0:
                        pool.wait_ge(o_norm, b * BLOCKS + BLOCKS)
                    pool.wait_ge(os_hi, b * NT + i + 1)
                    nc.gpsimd.tensor_tensor(oS[:, 1, :, cols], oT[:, :, cols],
                                            oS[:, 0, :, cols].bitcast(F32), ALU.subtract).then_inc(os_lo, 1)

        @block.scalar
        def _(act):
            with act.Fori(0, B) as b:
                def hi_of_ring(k, dst):
                    act.wait_ge(ring_filled, b * RING + k + 1)
                    nc.scalar.activation(dst, ring[:, k % 2, :], ACT.Copy).then_inc(ring_hi, 1)

                act.wait_ge(ve_done, b * 2 + 1)
                nc.scalar.activation(std[:, :], ve[:, :], ACT.Sqrt).then_inc(std_done, 1)
                for i in range(NT):
                    act.wait_ge(ring_filled, b * RING + ring_norm(i) + 1)
                    nc.scalar.activation(nT[:, 0, :, i * P:(i + 1) * P],
                                         ring[:, ring_norm(i) % 2, :].rearrange("p (k t) -> p k t", k=KC),
                                         ACT.Copy).then_inc(ring_hi, 1)
                for i in range(NT):
                    act.wait_ge(v_sum, b * NT + i + 1)
                    src = tok[:, i % 4, :].rearrange("p (a h d) -> p a h d", a=PAIRS, h=2)
                    nc.scalar.activation(V[:, i, :, 0:4:3, :], src, ACT.Copy).then_inc(v_hi, 1)
                for s in range(UNITS + 5):
                    if s < UNITS and s % UP == 0:
                        p = s // UP
                        for r in range(4):
                            k = ring_proj(p, r)
                            act.wait_ge(ring_filled, b * RING + k + 1)
                            nc.scalar.activation(qk[:, r // 2, 0, (r % 2) * 512:(r % 2) * 512 + 512],
                                                 ring[:, k % 2, :], ACT.Identity,
                                                 bias=bqk[:, r // 2, p:p + 1]).then_inc(ring_hi, 1)
                    if 1 <= s <= UNITS:
                        u = s - 1
                        for c in range(2):
                            k = ring_probs(u, c)
                            act.wait_ge(ring_filled, b * RING + k + 1)
                            if u // 2 >= 2 and u % 2 == 0 and c == 0:
                                act.wait_ge(pv_done, b * BLOCKS + u // 2 - 1)
                            nc.scalar.activation(PT[:, 0, u // 2 % 2, 4 * c:4 * c + 4, u % 2 * P:u % 2 * P + P],
                                                 ring[:, k % 2, :].rearrange("p (m q) -> p m q", m=4),
                                                 ACT.Copy).then_inc(ring_hi, 1)
                    if s < UNITS:
                        if s == 0:
                            act.wait_ge(v_lo, b * NT + NT)
                        if s >= 2:
                            act.wait_ge(ring_filled, b * RING + ring_probs(s - 2, 1) + 1)
                        act.wait_ge(max_done, b * UNITS + s + 1)
                        nc.scalar.activation(prob[:, s % 2, :], S[:, s % 2, :], ACT.Exp, bias=nmax[:, s:s + 1],
                                             accum_out=rsum[:, s:s + 1]).then_inc(exp_done, 1)
                    if s >= 5 and s % 2 == 1:
                        m = (s - 5) // 2
                        odd = m // (NT // 2) % 2
                        rows, other = slice(D * odd, D * odd + D), slice(D * (1 - odd), D * (1 - odd) + D)
                        act.wait_ge(pv_done, b * BLOCKS + m + 1)
                        if m >= 2:
                            act.wait_ge(o_norm, b * BLOCKS + m - 1)
                        nc.scalar.activation(Rs[rows, m % 2, :], O[rows, m % 2, QC:2 * QC], ACT.Copy)
                        nc.scalar.activation(oL[rows, m % 2, :], O[other, m % 2, 0:QC], ACT.Copy
                                             ).then_inc(o_copied, 1)
                for i in range(NT):
                    cols = slice(i * P, (i + 1) * P)
                    if i == 0:
                        act.wait_ge(o_norm, b * BLOCKS + BLOCKS)
                    nc.scalar.activation(oS[:, 0, :, cols], oT[:, :, cols], ACT.Copy).then_inc(os_hi, 1)
                act.wait_ge(ve_done, b * 2 + 2)
                nc.scalar.activation(std[:, :], ve[:, :], ACT.Sqrt).then_inc(std_done, 1)
                for i in range(NT):
                    act.wait_ge(n2_filled, b * NT + i + 1)
                    if i == 0:
                        act.wait_ge(os_lo, b * NT + NT)
                    nc.scalar.activation(n2T[:, i, :, :], S4[:, i % 4, :].rearrange("p (k t) -> p k t", k=KC),
                                         ACT.Copy).then_inc(n2_copied, 1)
                act.wait_ge(soft, b * 5 + 2)
                nc.scalar.activation(lg[:, :, :], lg[:, :, :], ACT.Exp).then_inc(soft_exp, 1)
                for i in range(2):
                    act.wait_ge(affT_filled, b * 2 + i + 1)
                    nc.scalar.activation(affT[:, 512 * i:512 * i + 512], O[0:E, 1 - i, :], ACT.Copy
                                         ).then_inc(affT_copied, 1)

        @block.vector
        def _(dve):
            for w in range(4):
                j = w % 2
                src = xt[:, KC * j:KC * j + KC, :].rearrange("p k c -> p (k c)")
                half = [oS[:, h, :, :].rearrange("p k n -> p (k n)")[:, j * KC * C:(j + 1) * KC * C] for h in range(2)]
                if j == 0:
                    dve.wait_ge(w_raw_in, 16 * (w + 2))
                if w == 2:
                    dve.wait_ge(w_out, 16 * 4 * PAIRS)
                scale = D ** -0.5 if w == 0 else 1.0
                nc.vector.tensor_scalar(half[0], src, scale, None, ALU.mult).then_inc(w_hi, 1)
                dve.wait_ge(w_hi, w + 1)
                nc.vector.scalar_tensor_tensor(out=half[1], in0=src, scalar=scale, in1=half[0].bitcast(F32),
                                               op0=ALU.mult, op1=ALU.subtract).then_inc(w_lo, 1)
            dve.wait_ge(consts_in, 64)
            nc.vector.tensor_scalar(bqk[:, 0, :], bqk[:, 0, :], D ** -0.5, None, ALU.mult).then_inc(bq_scaled, 1)
            dve.wait_ge(bq_scaled, 1)
            dve.wait_ge(w_out, 16 * (4 * PAIRS + 4))

            with dve.Fori(0, B) as b:
                def rstd_of(n, eps):
                    nc.vector.tensor_scalar(ve[:, :], mv[:, :, 1], eps, None, ALU.add).then_inc(ve_done, 1)
                    dve.wait_ge(std_done, b * 2 + n + 1)
                    nc.vector.reciprocal(r0[:, :], std[:, :]).then_inc(newton, 1)
                    dve.wait_ge(newton, b * 10 + n * 5 + 1)
                    nc.vector.tensor_tensor(r1[:, :], r0[:, :], r0[:, :], ALU.mult).then_inc(newton, 1)
                    dve.wait_ge(newton, b * 10 + n * 5 + 2)
                    nc.vector.tensor_tensor(rstd[:, :], r1[:, :], ve[:, :], ALU.mult).then_inc(newton, 1)
                    dve.wait_ge(newton, b * 10 + n * 5 + 3)
                    nc.vector.tensor_scalar(r1[:, :], rstd[:, :], -0.5, 1.5, ALU.mult, ALU.add).then_inc(newton, 1)
                    dve.wait_ge(newton, b * 10 + n * 5 + 4)
                    nc.vector.tensor_tensor(rstd[:, :], r0[:, :], r1[:, :], ALU.mult).then_inc(newton, 1)
                    dve.wait_ge(newton, b * 10 + n * 5 + 5)

                def aggregate(n):
                    dve.wait_ge(stats_done, b * (2 * NT) + n * NT + NT)
                    dve.sem_inc(dve_passed, 1)
                    for i in range(NT):
                        last = nc.vector.bn_aggr(mv[:, i, :], stats[:, i, :])
                    last.then_inc(mv_done, 1)
                    dve.wait_ge(mv_done, b * 2 + n + 1)

                def normalise(i):
                    return nc.vector.tensor_scalar(tok[:, i % 4, :], xt[:, i, :], mv[:, i, 0:1],
                                                   rstd[:, i:i + 1], ALU.subtract, ALU.mult)

                for i in range(NT):
                    if i % 4 == 0:
                        dve.wait_ge(x_in[i // 4], b * 16 + 16)
                    nc.vector.bn_stats(stats[:, i, :], xt[:, i, :]).then_inc(stats_done, 1)
                aggregate(0)
                rstd_of(0, EPS1)
                for i in range(NT + 2):
                    if i < NT:
                        if i >= 4:
                            dve.wait_ge(ring_filled, b * RING + ring_norm(i - 4) + 1)
                        normalise(i).then_inc(norm_done, 1)
                    if i >= 2:
                        k = ring_norm(i - 2)
                        dve.wait_ge(ring_hi, b * RING + k + 1)
                        nc.vector.tensor_tensor(nT[:, 1, :, (i - 2) * P:(i - 1) * P],
                                                ring[:, k % 2, :].rearrange("p (k t) -> p k t", k=KC),
                                                nT[:, 0, :, (i - 2) * P:(i - 1) * P].bitcast(F32),
                                                ALU.subtract).then_inc(ring_lo, 1)
                for i in range(NT):
                    dve.wait_ge(o_filled, b * (2 * NT) + i + 1)
                    if i >= 4:
                        dve.wait_ge(v_lo, b * NT + i - 3)
                    nc.vector.tensor_tensor(tok[:, i % 4, :], O[:, i % 2, :], bv_bc[:, :], ALU.add
                                            ).then_inc(v_sum, 1)
                for s in range(UNITS + 5):
                    if s < UNITS and s % UP == 0:
                        p = s // UP
                        for r in range(4):
                            k = ring_proj(p, r)
                            cols = slice((r % 2) * 512, (r % 2) * 512 + 512)
                            dve.wait_ge(ring_hi, b * RING + k + 1)
                            nc.vector.scalar_tensor_tensor(
                                out=qk[:, r // 2, 1, cols], in0=ring[:, k % 2, :], scalar=bqk[:, r // 2, p:p + 1],
                                in1=qk[:, r // 2, 0, cols].bitcast(F32), op0=ALU.add, op1=ALU.subtract
                            ).then_inc(ring_lo, 1)
                    if s < UNITS:
                        dve.wait_ge(s_filled, b * UNITS + s + 1)
                        nc.vector.tensor_reduce(nmax[:, s:s + 1], S[:, s % 2, :], AX.X, ALU.max, negate=True
                                                ).then_inc(max_done, 1)
                    if s >= 6 and s % 2 == 0:
                        m = (s - 6) // 2
                        odd = m // (NT // 2) % 2
                        rows = slice(D * odd, D * odd + D)
                        dve.wait_ge(o_copied, b * BLOCKS + m + 1)
                        nc.vector.tensor_tensor(oSum[rows, m % 2, :], O[rows, m % 2, 0:QC], oL[rows, m % 2, :],
                                                ALU.add).then_inc(o_sum, 1)
                    if 1 <= s <= UNITS:
                        u = s - 1
                        for c in range(2):
                            k = ring_probs(u, c)
                            here = (u // 2 % 2, slice(4 * c, 4 * c + 4), slice(u % 2 * P, u % 2 * P + P))
                            dve.wait_ge(ring_hi, b * RING + k + 1)
                            nc.vector.tensor_tensor(PT[:, 1, here[0], here[1], here[2]],
                                                    ring[:, k % 2, :].rearrange("p (m q) -> p m q", m=4),
                                                    PT[:, 0, here[0], here[1], here[2]].bitcast(F32),
                                                    ALU.subtract).then_inc(ring_lo, 1)
                        if u % 2 == 1:
                            dve.wait_ge(exp_done, b * UNITS + u + 1)
                            nc.vector.reciprocal(rinv[:, u - 1:u + 1], rsum[:, u - 1:u + 1]).then_inc(rinv_done, 1)
                for i in range(NT):
                    dve.wait_ge(o_filled, b * (2 * NT) + NT + i + 1)
                    dve.wait_ge(xbo, b * NT + i + 1)
                    nc.vector.tensor_tensor(xt[:, i, :], O[:, i % 2, :], xt[:, i, :], ALU.add).then_inc(t_done, 1)
                    dve.wait_ge(t_done, b * NT + i + 1)
                    nc.vector.bn_stats(stats[:, i, :], xt[:, i, :]).then_inc(stats_done, 1)
                aggregate(1)
                rstd_of(1, EPS2)
                for i in range(NT):
                    if i >= 4:
                        dve.wait_ge(n2_filled, b * NT + i - 3)
                        dve.wait_ge(n2_out[i % 4], b * (4 * NT) + 16 * (i // 4))
                    normalise(i).then_inc(norm_done, 1)
                dve.wait_ge(logits, b * 1 + 1)
                lgp = O[:, 0, 0:NT * E].rearrange("p (i e) -> p i e", e=E)
                nc.vector.tensor_reduce(gmax[:, :], lgp, AX.X, ALU.max).then_inc(soft, 1)
                dve.wait_ge(soft, b * 5 + 1)
                nc.vector.tensor_tensor(lg[:, :, :], lgp, gmax[:, :].unsqueeze(2).broadcast_to([P, NT, E]),
                                        ALU.subtract).then_inc(soft, 1)
                dve.wait_ge(soft_exp, b * 1 + 1)
                nc.vector.tensor_reduce(gsum[:, :], lg[:, :, :], AX.X, ALU.add).then_inc(soft, 1)
                dve.wait_ge(soft, b * 5 + 3)
                nc.vector.reciprocal(grec[:, :], gsum[:, :]).then_inc(soft, 1)
                dve.wait_ge(soft, b * 5 + 4)
                nc.vector.tensor_tensor(aff[:, :, :], lg[:, :, :], grec[:, :].unsqueeze(2).broadcast_to([P, NT, E]),
                                        ALU.mult).then_inc(soft, 1)

        @block.tensor
        def _(pe):
            def products(dst, pairs):
                for n, (l, r) in enumerate(pairs):
                    last = nc.tensor.matmul(dst, l, r, start=(n == 0), stop=(n == len(pairs) - 1))
                return last

            HL = [(0, 0), (0, 1), (1, 0)]
            pe.wait_ge(consts_in, 64)
            with pe.Fori(0, B) as b:
                for i in range(NT):
                    k = ring_norm(i)
                    pe.wait_ge(norm_done, b * (2 * NT) + i + 1)
                    if i >= 2:
                        pe.wait_ge(ring_lo, b * RING + k - 1)
                    for c in range(KC):
                        last = nc.tensor.transpose(ring[:, k % 2, c * P:(c + 1) * P],
                                                   tok[:, i % 4, c * P:(c + 1) * P], ident)
                    last.then_inc(ring_filled, 1)
                pe.wait_ge(wv_in, b * 16 + 16)
                for i in range(NT):
                    pe.wait_ge(ring_lo, b * RING + ring_norm(i) + 1)
                    if i >= 2:
                        pe.wait_ge(v_sum, b * NT + i - 1)
                    products(O[:, i % 2, :], [(nT[:, l, c, i * P:(i + 1) * P], wvo[:, w, c, :])
                                              for c in range(KC) for l, w in HL]).then_inc(o_filled, 1)
                for s in range(UNITS + 5):
                    if s < UNITS and s % UP == 0:
                        p = s // UP
                        pe.wait_ge(wqk_in[p % 2], b * 32 + 16 * (p // 2) + 16)
                        for r in range(4):
                            k = ring_proj(p, r)
                            pe.wait_ge(ring_lo, b * RING + k - 1)
                            products(ring[:, k % 2, :],
                                     [(wqk[:, p % 2, 2 * (r // 2) + w, c, :],
                                       nT[:, l, c, (r % 2) * 512:(r % 2) * 512 + 512])
                                      for c in range(KC) for w, l in HL]).then_inc(ring_filled, 1)
                        pe.wait_ge(ring_lo, b * RING + ring_proj(p, 3) + 1)
                    if s < UNITS:
                        odd, i = s // NT % 2, s % NT
                        rows = slice(D * odd, D * odd + D)
                        if s >= 2:
                            pe.wait_ge(exp_done, b * UNITS + s - 1)
                        for l in range(2):
                            for m in range(2):
                                for r in range(2 - l):
                                    last = nc.tensor.matmul(S[:, s % 2, 512 * m:512 * m + 512],
                                                            qk[rows, 0, l, i * P:(i + 1) * P],
                                                            qk[rows, 1, r, 512 * m:512 * m + 512],
                                                            start=(l + r == 0), stop=(l == 1))
                        last.then_inc(s_filled, 1)
                    if s >= 4 and (s - 4) // 2 < BLOCKS:
                        m, part = (s - 4) // 2, s % 2
                        head = m // (NT // 2)
                        if part == 0:
                            if m == 0:
                                pe.wait_ge(v_lo, b * NT + NT)
                            if m >= 2:
                                pe.wait_ge(o_sum, b * BLOCKS + m - 1)
                            pe.wait_ge(ring_lo, b * RING + ring_probs(2 * m + 1, 1) + 1)
                        for t in range(4 * part, 4 * part + 4):
                            for l in range(2):
                                nc.tensor.matmul(
                                    O[:, m % 2, 0:QC],
                                    V[:, t, head // 2, 2 * (head % 2):2 * (head % 2) + 2, :].rearrange("p h d -> p (h d)"),
                                    PT[:, l, m % 2, t, :],
                                    start=(t + l == 0), stop=(t == NT - 1 and l == 1))
                        if part == 1:
                            pe.wait_ge(rbc_done, b * BLOCKS + m + 1)
                            for j in range(2):
                                last = nc.tensor.transpose(O[:, m % 2, QC + j * P:QC + (j + 1) * P],
                                                           rinv_bc[:, m % 2, j, :], ident)
                            last.then_inc(pv_done, 1)
                    if 1 <= s <= UNITS:
                        u = s - 1
                        for c in range(2):
                            k = ring_probs(u, c)
                            if c == 0:
                                pe.wait_ge(exp_done, b * UNITS + u + 1)
                            pe.wait_ge(ring_lo, b * RING + k - 1)
                            for m in range(4):
                                last = nc.tensor.transpose(ring[:, k % 2, m * P:(m + 1) * P],
                                                           prob[:, u % 2, (4 * c + m) * P:(4 * c + m + 1) * P], ident)
                            last.then_inc(ring_filled, 1)
                pe.wait_ge(wo_in, b * 16 + 16)
                pe.wait_ge(o_sum, b * BLOCKS + BLOCKS)
                for i in range(NT):
                    pe.wait_ge(os_lo, b * NT + i + 1)
                    if i >= 2:
                        pe.wait_ge(t_done, b * NT + i - 1)
                    products(O[:, i % 2, :], [(oS[:, l, c, i * P:(i + 1) * P], wvo[:, w, c, :])
                                              for c in range(KC) for l, w in HL]).then_inc(o_filled, 1)
                pe.wait_ge(t_done, b * NT + NT)
                for i in range(NT + 1):
                    if i < NT:
                        pe.wait_ge(norm_done, b * (2 * NT) + NT + i + 1)
                        if i >= 4:
                            pe.wait_ge(n2_copied, b * NT + i - 3)
                        for c in range(KC):
                            last = nc.tensor.transpose(S4[:, i % 4, c * P:(c + 1) * P],
                                                       tok[:, i % 4, c * P:(c + 1) * P], ident)
                        last.then_inc(n2_filled, 1)
                    if i >= 1:
                        pe.wait_ge(n2_copied, b * NT + i)
                        last = products(O[:, 0, (i - 1) * E:i * E],
                                        [(n2T[:, i - 1, c, :], gate_sb[:, c, :]) for c in range(KC)])
                last.then_inc(logits, 1)
                pe.wait_ge(soft, b * 5 + 5)
                for h in range(2):
                    for i in range(4):
                        last = nc.tensor.transpose(O[0:E, 1 - h, i * P:(i + 1) * P], aff[:, 4 * h + i, :], ident)
                    last.then_inc(affT_filled, 1)


def program(nc, out, x, wT, b_row, b_col, gate, w1, w2, b1, b2):
    n2 = nc.dram_tensor("n2_rows", [B, N, C], F32).ap()
    aff = nc.dram_tensor("affinities", [B, E, N], F32).ap()
    with ExitStack() as ctx:
        ident = ctx.enter_context(nc.sbuf_tensor("ident", [P, P], F32))
        idx = ctx.enter_context(nc.sbuf_tensor("idx", [P, E * B], U32))
        gates = ctx.enter_context(nc.sbuf_tensor("gates", [P, E * B], F32))
        ident_made = ctx.enter_context(nc.semaphore("ident_made"))
        with nc.Block() as block:
            @block.gpsimd
            def _(pool):
                nc.gpsimd.memset(ident[:, :], 0.0).then_inc(ident_made, 1)
                pool.wait_ge(ident_made, 1)
                nc.gpsimd.affine_select(out=ident[:, :], in_=ident[:, :], compare_op=ALU.not_equal, fill=1.0,
                                        base=0, pattern=[[-1, P]], channel_multiplier=1).then_inc(ident_made, 1)
                pool.wait_ge(ident_made, 2)
        attention(nc, x, wT, b_row, b_col, gate, out, n2, aff, ident[:, :])
        choose_tokens(nc, aff, ident[:, :], idx[:, :], gates[:, :])
        experts(nc, w1, w2, b1, b2, out.rearrange("b n c -> (b n) c"), n2.rearrange("b n c -> (b n) c"),
                ident[:, :], idx[:, :], gates[:, :])


def choose_tokens(nc, aff_dram, ident, idx, gates):
    with ExitStack() as ctx:
        def sb(name, shape, dt=F32):
            return ctx.enter_context(nc.sbuf_tensor(name, shape, dt))

        def sem(name):
            return ctx.enter_context(nc.semaphore(name))

        work = sb("work", [P, 2, N])
        top8 = sb("top8", [P, CAP])
        pos = sb("pos", [P, CAP], U32)
        posf = sb("posf", [P, CAP])
        rowf = sb("rowf", [P, CAP])
        base_i = sb("base_i", [P, B, E], mybir.dt.int32)
        base_f = sb("base_f", [P, B, E])
        pt = ctx.enter_context(nc.psum_tensor("pt", [P, 2, 512], F32))
        aff_in = sem("aff_in")
        base_made = sem("base_made")
        picked = sem("picked")
        rows_made = sem("rows_made")
        turned = sem("turned")
        copied = sem("copied")
        block = ctx.enter_context(nc.Block())
        STEPS = CAP // 8

        @block.sync
        def _(sp):
            sp.dma_start(work[:, 0, :], aff_dram.rearrange("b e n -> (b e) n")).then_inc(aff_in, 16)

        @block.gpsimd
        def _(pool):
            nc.gpsimd.iota(base_i[:, :, :], pattern=[[N, B], [0, E]], base=0, channel_multiplier=0
                           ).then_inc(base_made, 1)

        @block.vector
        def _(dve):
            dve.wait_ge(aff_in, 16)
            for r in range(STEPS):
                src, dst = work[:, r % 2, :], work[:, 1 - r % 2, :]
                best = top8[:, 8 * r:8 * r + 8]
                nc.vector.max(best, src).then_inc(picked, 1)
                dve.wait_ge(picked, 2 * r + 1)
                nc.vector.max_index(pos[:, 8 * r:8 * r + 8], best, src)
                nc.vector.match_replace(dst, best, src, -1.0).then_inc(picked, 1)
                dve.wait_ge(picked, 2 * r + 2)
            nc.vector.tensor_copy(posf[:, :], pos[:, :]).then_inc(rows_made, 1)
            dve.wait_ge(base_made, 1)
            nc.vector.tensor_copy(base_f[:, :, :], base_i[:, :, :]).then_inc(rows_made, 1)
            dve.wait_ge(rows_made, 2)
            dve.wait_ge(turned, 1)
            nc.vector.tensor_tensor(idx.rearrange("p (e b) -> p b e", e=E),
                                    pt[:, 0, 0:P].rearrange("p (b e) -> p b e", e=E), base_f[:, :, :],
                                    ALU.add).then_inc(copied, 1)
            dve.wait_ge(turned, 2)
            nc.vector.tensor_copy(gates.rearrange("p (e b) -> p b e", e=E),
                                  pt[:, 1, 0:P].rearrange("p (b e) -> p b e", e=E)).then_inc(copied, 1)
            dve.wait_ge(copied, 2)

        @block.tensor
        def _(pe):
            pe.wait_ge(rows_made, 1)
            nc.tensor.transpose(pt[:, 0, 0:P], posf[:, :], ident).then_inc(turned, 1)
            nc.tensor.transpose(pt[:, 1, 0:P], top8[:, :], ident).then_inc(turned, 1)


def experts(nc, w1, w2, b1, b2, out_rows, n2_rows, ident, idx, gates):
    G = 4
    COLS = G * CAP
    with ExitStack() as ctx:
        def sb(name, shape, dt=F32):
            return ctx.enter_context(nc.sbuf_tensor(name, shape, dt))

        def sem(name):
            return ctx.enter_context(nc.semaphore(name))

        wraw = sb("wraw", [P, 2 * KC, FF])
        ws = sb("ws", [P, 2, 2, 2 * KC, FF], F32R)
        b1s = sb("b1s", [P, 2, KC])
        b2s = sb("b2s", [P, 2, C])
        idxc = sb("idxc", [P, 2, B], U32)
        gatec = sb("gatec", [P, 2, B])
        xg = sb("xg", [P, 2, G, C])
        xT = sb("xT", [P, 2, 2, KC, COLS], F32R)
        hf = sb("hf", [P, 2, COLS])
        hT = sb("hT", [P, 2, KC, COLS], F32R)
        y0 = sb("y0", [P, 2, C])
        y = sb("y", [P, 2, G, C])
        xr = ctx.enter_context(nc.psum_tensor("xr", [P, 2, 512], F32))
        p1 = ctx.enter_context(nc.psum_tensor("p1", [P, 2, 512], F32))
        p2 = ctx.enter_context(nc.psum_tensor("p2", [P, 4, 512], F32))

        w_in = sem("w_in")
        b12_in = [sem(f"b12_in{i}") for i in range(2)]
        ws_hi = sem("ws_hi")
        ws_lo = sem("ws_lo")
        cols_made = sem("cols_made")
        gathered = [sem(f"gathered{i}") for i in range(2)]
        xr_filled = sem("xr_filled")
        xr_hi = sem("xr_hi")
        xr_lo = sem("xr_lo")
        p1_filled = sem("p1_filled")
        h_done = sem("h_done")
        h_hi = sem("h_hi")
        h_lo = sem("h_lo")
        p2_filled = sem("p2_filled")
        y0_done = sem("y0_done")
        y_done = sem("y_done")
        added = [sem(f"added{i}") for i in range(B)]
        sp_passed2, pool_passed2 = sem("sp_passed2"), sem("pool_passed2")
        block = ctx.enter_context(nc.Block())
        WCH = 2 * KC

        def every_expert(engine, expert):
            expert(0, 0, False)
            expert(1, 1, False)
            with engine.Fori(1, E // 2 - 1) as twos:
                expert(2 * twos, 0, False)
                expert(2 * twos + 1, 1, False)
            expert(E - 2, 0, False)
            expert(E - 1, 1, True)

        def started(e, g, n):
            return type(e) is not int or e > 0 or g > 0 or n >= 0

        @block.sync
        def _(sp):
            def load(e, k):
                sp.dma_start(wraw[:, 0:KC, :], w1[e]).then_inc(w_in, 16)
                sp.dma_start(wraw[:, KC:2 * KC, :], w2[e]).then_inc(w_in, 16)
                sp.dma_start(b1s[:, k, :], b1[e]).then_inc(b12_in[k], 16)
                sp.dma_start(b2s[:, k, :], b2[e].broadcast_to([P, C])).then_inc(b12_in[k], 16)

            load(0, 0)
            sp.wait_ge(ws_lo, WCH)
            load(1, 1)
            with sp.Fori(0, E // 2 - 1) as twos:
                for k in range(2):
                    e = 2 * twos
                    sp.wait_ge(ws_lo, (e + k) * WCH + 2 * WCH)
                    sp.sem_inc(sp_passed2, 1)
                    sp.wait_ge(y0_done, (e + k) * (2 * G) + 2 * G)
                    load(e + k + 2, k)

        @block.gpsimd
        def _(pool):
            def columns(e, k):
                nc.gpsimd.tensor_copy(idxc[:, k, :], idx[:, bass.ds(e * B, B)])
                nc.gpsimd.tensor_copy(gatec[:, k, :], gates[:, bass.ds(e * B, B)]).then_inc(cols_made, 1)

            def gather(k, g):
                for j in range(G):
                    pool.indirect_dma_start(
                        out=xg[:, g, j, :], out_offset=None, in_=n2_rows,
                        in_offset=bass.IndirectOffsetOnAxis(ap=idxc[:, k, G * g + j:G * g + j + 1], axis=0),
                    ).then_inc(gathered[g], 16)

            def scatter(e, k, g):
                for j in range(G):
                    pool.wait_ge(y_done, e * (2 * G) + G * g + j + 1)
                    if type(e) is not int or e > 0:
                        pool.wait_ge(added[G * g + j], e * 16)
                    pool.sem_inc(pool_passed2, 1)
                    pool.indirect_dma_start(
                        out=out_rows, out_offset=bass.IndirectOffsetOnAxis(ap=idxc[:, k, G * g + j:G * g + j + 1], axis=0),
                        in_=y[:, g, j, :], in_offset=None, compute_op=ALU.add,
                    ).then_inc(added[G * g + j], 16)

            def expert(e, k, last):
                if not last:
                    if type(e) is not int or e > 0:
                        pool.wait_ge(y_done, e * (2 * G))
                        for i in range(B):
                            pool.wait_ge(added[i], e * 16)
                    columns(e + 1, 1 - k)
                    pool.wait_ge(cols_made, e + 2)
                for g in range(2):
                    if not last:
                        pool.wait_ge(xr_filled, e * (2 * G) + G * g + G)
                        pool.sem_inc(pool_passed2, 1)
                        gather(1 - k, g)
                    scatter(e, k, g)

            columns(0, 0)
            pool.wait_ge(cols_made, 1)
            gather(0, 0)
            gather(0, 1)
            every_expert(pool, expert)
            for i in range(B):
                pool.wait_ge(added[i], 16 * E)

        @block.scalar
        def _(act):
            def turn(v, g):
                for j in range(G):
                    act.wait_ge(xr_filled, v * G + j + 1)
                    nc.scalar.activation(xT[:, g, 0, :, j * P:(j + 1) * P],
                                         xr[:, j % 2, :].rearrange("p (k t) -> p k t", k=KC),
                                         ACT.Copy).then_inc(xr_hi, 1)

            def expert(e, k, last):
                act.wait_ge(b12_in[k], (e - k) * 16 + 32)
                act.wait_ge(cols_made, e + 1)
                for g in range(2):
                    v = e * 2 + g
                    for m in range(KC):
                        act.wait_ge(p1_filled, v * KC + m + 1)
                        if started(e, g, m - 2):
                            act.wait_ge(h_lo, v * KC + m - 1)
                        nc.scalar.activation(hf[:, m % 2, :], p1[:, m % 2, :], ACT.Gelu_apprx_tanh,
                                             bias=b1s[:, k, m:m + 1]).then_inc(h_done, 1)
                    if not (last and g == 1):
                        turn(v + 1, 1 - g)
                    for j in range(G):
                        act.wait_ge(y0_done, v * G + j + 1)
                        if started(e, 0, -1):
                            act.wait_ge(added[G * g + j], e * 16)
                        nc.scalar.activation(y[:, g, j, :], y0[:, j % 2, :], ACT.Copy,
                                             scale=gatec[:, k, G * g + j:G * g + j + 1]).then_inc(y_done, 1)

            turn(0, 0)
            every_expert(act, expert)

        @block.vector
        def _(dve):
            def split_chunk(e, k, c):
                if c == 0:
                    dve.wait_ge(w_in, e * 32 + 32)
                nc.vector.tensor_copy(ws[:, k, 0, c, :], wraw[:, c, :]).then_inc(ws_hi, 1)
                dve.wait_ge(ws_hi, e * WCH + c + 1)
                nc.vector.tensor_tensor(ws[:, k, 1, c, :], wraw[:, c, :], ws[:, k, 0, c, :].bitcast(F32),
                                        ALU.subtract).then_inc(ws_lo, 1)

            def turn(v, g):
                for j in range(G):
                    dve.wait_ge(xr_hi, v * G + j + 1)
                    nc.vector.tensor_tensor(xT[:, g, 1, :, j * P:(j + 1) * P],
                                            xr[:, j % 2, :].rearrange("p (k t) -> p k t", k=KC),
                                            xT[:, g, 0, :, j * P:(j + 1) * P].bitcast(F32),
                                            ALU.subtract).then_inc(xr_lo, 1)

            def expert(e, k, last):
                dve.wait_ge(b12_in[k], (e - k) * 16 + 32)
                for g in range(2):
                    v = e * 2 + g
                    for m in range(KC):
                        dve.wait_ge(h_done, v * KC + m + 1)
                        if m == 0 and started(e, g, -1):
                            dve.wait_ge(p2_filled, v * G)
                        nc.vector.tensor_copy(hT[:, 0, m, :], hf[:, m % 2, :]).then_inc(h_hi, 1)
                        dve.wait_ge(h_hi, v * KC + m + 1)
                        nc.vector.tensor_tensor(hT[:, 1, m, :], hf[:, m % 2, :], hT[:, 0, m, :].bitcast(F32),
                                                ALU.subtract).then_inc(h_lo, 1)
                    if not (last and g == 1):
                        turn(v + 1, 1 - g)
                    for j in range(G):
                        dve.wait_ge(p2_filled, v * G + j + 1)
                        if started(e, g, j - 2):
                            dve.wait_ge(y_done, v * G + j - 1)
                        nc.vector.tensor_tensor(y0[:, j % 2, :], p2[:, j, :], b2s[:, k, :], ALU.add
                                                ).then_inc(y0_done, 1)
                    if not last:
                        for c in range(4 * g, 4 * g + 4):
                            split_chunk(e + 1, 1 - k, c)

            for c in range(WCH):
                split_chunk(0, 0, c)
            turn(0, 0)
            every_expert(dve, expert)

        @block.tensor
        def _(pe):
            HL = [(0, 0), (0, 1), (1, 0)]

            def products(dst, pairs):
                for n, (l, r) in enumerate(pairs):
                    last = nc.tensor.matmul(dst, l, r, start=(n == 0), stop=(n == len(pairs) - 1))
                return last

            def turn(e, v, g):
                pe.wait_ge(gathered[g], e * (16 * G) + 16 * G)
                for j in range(G):
                    if type(v) is not int or v > 0 or j >= 2:
                        pe.wait_ge(xr_lo, v * G + j - 1)
                    for c in range(KC):
                        last = nc.tensor.transpose(xr[:, j % 2, c * P:(c + 1) * P], xg[:, g, j, c * P:(c + 1) * P],
                                                   ident)
                    last.then_inc(xr_filled, 1)

            def expert(e, k, last):
                pe.wait_ge(ws_lo, e * WCH + WCH)
                for g in range(2):
                    v = e * 2 + g
                    pe.wait_ge(xr_lo, v * G + G)
                    for m in range(KC):
                        if started(e, g, m - 2):
                            pe.wait_ge(h_done, v * KC + m - 1)
                        products(p1[:, m % 2, :], [(ws[:, k, w, c, m * P:(m + 1) * P], xT[:, g, l, c, :])
                                                   for c in range(KC) for w, l in HL]).then_inc(p1_filled, 1)
                    if not (last and g == 1):
                        turn(e + g, v + 1, 1 - g)
                    for j in range(G):
                        if j == 0:
                            pe.wait_ge(h_lo, v * KC + KC)
                        if started(e, g, -1):
                            pe.wait_ge(y0_done, v * G + j - 3)
                        products(p2[:, j, :], [(hT[:, l, c, j * P:(j + 1) * P], ws[:, k, w, KC + c, :])
                                               for c in range(KC) for l, w in HL]).then_inc(p2_filled, 1)

            turn(0, 0, 0)
            every_expert(pe, expert)


_OUT = "out_dram"


def kernel(**inputs):
    import numpy as np
    import concourse.bacc as bacc
    from concourse.bass_utils import run_bass_kernel_spmd

    nc = bacc.Bacc("TRN2", target_bir_lowering=False, num_devices=1)
    a = {k: np.asarray(v) for k, v in inputs.items()}

    def chunks(w):
        return w.reshape(*w.shape[:-2], KC, P, w.shape[-1]).swapaxes(-3, -2)

    biases = [a["L0_conv_bq"], a["L0_conv_bk"], a["L0_conv_bv"], a["L0_conv_bo"]]
    arrays = {
        "x_dram": a["x"].reshape(B, C, N).transpose(0, 2, 1),
        "wT_dram": np.stack([chunks(a["L0_conv_" + n].T) for n in ("Wq", "Wk", "Wv", "Wo")]),
        "b_row_dram": np.stack(biases),
        "b_col_dram": np.stack([v.reshape(KC, P).T for v in biases[:2]], 1),
        "gate_dram": chunks(a["L0_ffn_gate_weight"]),
        "w1_dram": chunks(a["L0_ffn_w1"]),
        "w2_dram": chunks(a["L0_ffn_w2"]),
        "b1_dram": a["L0_ffn_b1"].reshape(E, KC, P).transpose(0, 2, 1),
        "b2_dram": a["L0_ffn_b2"].reshape(E, 1, C),
    }
    arrays = {k: np.ascontiguousarray(v) for k, v in arrays.items()}
    d = {k: nc.dram_tensor(k, v.shape, F32, kind="ExternalInput").ap() for k, v in arrays.items()}
    out = nc.dram_tensor(_OUT, (B, N, C), F32, kind="ExternalOutput").ap()
    program(nc, out, **{k.removesuffix("_dram"): v for k, v in d.items()})
    r = run_bass_kernel_spmd(nc, [arrays], core_ids=[0])
    return np.ascontiguousarray(r.results[0][_OUT].transpose(0, 2, 1)).reshape(B, C, 32, 32)
```

```python
from contextlib import ExitStack

import concourse.bass as bass
from concourse import mybir

F32 = mybir.dt.float32
F32R = mybir.dt.float32r
U32 = mybir.dt.uint32
ACT = mybir.ActivationFunctionType
ALU = mybir.AluOpType
AX = mybir.AxisListType

P = 128
B, C, N = 8, 512, 1024
NT = N // P
KC = C // P
H, D = 8, 64
PAIRS = H // 2
E, FF = 16, 512
CAP = N // E * 2
EPS1, EPS2 = 1e-6, 1e-5

UP = 2 * NT
UNITS = PAIRS * UP
BLOCKS = UNITS // 2
QC = 2 * P

RING = NT + PAIRS * 4 + 2 * UNITS


def ring_norm(i):
    return i


def ring_proj(p, r):
    return NT + 4 * p + (2 * (UP * p - 1) if p else 0) + r


def ring_probs(u, c):
    return NT + 4 * min(PAIRS, (u + 1) // UP + 1) + 2 * u + c


def split_weights_dram(nc):
    wqk = nc.dram_tensor("wqk_split", [PAIRS, P, 4, KC, P], F32).ap()
    wv = nc.dram_tensor("wv_split", [P, 2, KC, C], F32).ap()
    return wqk, wv


EARLY_AT = [50, 51, 52, 53, 55, 56]

WRAP = [("norm", 0), ("root", 0), ("t", 4), ("norm", 1), ("n2", 0), ("t", 5), ("norm", 2), ("n2", 1),
        ("t", 6), ("norm", 3), ("n2", 2), ("t", 7), ("norm", 4), ("n2", 3), ("v", 0), ("root", 1), ("norm", 5),
        ("v", 1), ("n2", 4), ("norm", 6), ("v", 2), ("n2", 5), ("norm", 7), ("v", 3), ("n2", 6), ("v", 4),
        ("n2", 7), ("v", 5), ("v", 6), ("v", 7)]


def attention(nc, x, wT, b_row, b_col, gate, out, n2_dram, aff_dram, ident):
    wqk_dram, wv_dram = split_weights_dram(nc)
    with ExitStack() as ctx:
        def sb(name, shape, dt=F32):
            return ctx.enter_context(nc.sbuf_tensor(name, shape, dt))

        def sem(name):
            return ctx.enter_context(nc.semaphore(name))

        wqk = sb("wqk", [P, 2, 4, KC, P], F32R)
        wv = wqk[:, :, :, :, :].rearrange("p s w k c -> p s (w k c)").rearrange(
            "p h (k c) -> p h k c", k=KC)
        wo = sb("wo", [P, 2, KC, C], F32R)
        xt = sb("xt", [P, NT, C])
        nT = sb("nT", [P, 2, KC, N], F32R)
        oS = nT
        qk = sb("qk", [P, 2, 2, N], F32R)
        V = sb("V", [P, NT, PAIRS, 4, D], F32R)
        prob = sb("prob", [P, 2, N])
        tok = prob[:, :, :].rearrange("p a (s c) -> p (a s) c", c=C)
        PT = sb("PT", [P, 2, 2, NT, QC], F32R)
        oT = sb("oT", [P, KC, N])
        spare = sb("spare", [P, 2, C])

        def res(i):
            return oT[:, i // 2, (i % 2) * C:(i % 2) * C + C] if i < 6 else spare[:, i - 6, :]

        affT = oT[0:E, KC - 1, :]
        tmp = sb("tmp", [P, 3, 2, QC])
        Rs = tmp[:, 0, :, :]
        oL = tmp[:, 1, :, :]
        oSum = tmp[:, 2, :, :]
        n2T = tmp[:, 0:2, :, :].rearrange("p a q c -> p a (q c)").rearrange(
            "p a (k t) -> p a k t", k=KC)
        bv_bc = sb("bv_bc", [P, C])
        bo_bc = sb("bo_bc", [P, C])
        bqk = sb("bqk", [P, 2, KC])
        gate_sb = sb("gate_sb", [P, KC, E])
        nmax = sb("nmax", [P, UNITS])
        rsum = sb("rsum", [P, UNITS])
        rinv = sb("rinv", [P, UNITS])
        ones = sb("ones", [P, P])
        rinv_bc = sb("rinv_bc", [P, 2, 2, P])
        stats = sb("stats", [P, 2, NT, 6])
        mv = sb("mv", [P, 2, NT, 2])
        ve = sb("ve", [P, 2, NT])
        std = sb("std", [P, 2, NT])
        r0 = sb("r0", [P, NT])
        r1 = sb("r1", [P, NT])
        rstd = sb("rstd", [P, 2, NT])
        lg = sb("lg", [P, NT, E])
        aff = sb("aff", [P, NT, E])
        gmax = sb("gmax", [P, NT])
        gsum = sb("gsum", [P, NT])
        grec = sb("grec", [P, NT])

        S = ctx.enter_context(nc.psum_tensor("S", [P, 2, N], F32))
        ring = ctx.enter_context(nc.psum_tensor("ring", [P, 2, 512], F32))
        O = ctx.enter_context(nc.psum_tensor("O", [P, 2, 512], F32))
        S4 = S[:, :, :].rearrange("p a (h n) -> p (a h) n", h=2)

        wv_raw_in = sem("wv_raw_in")
        wqk_raw_in = sem("wqk_raw_in")
        wo_raw_in = sem("wo_raw_in")
        w_hi = sem("w_hi")
        w_lo = sem("w_lo")
        wv_out = sem("wv_out")
        w0_out = sem("w0_out")
        w_out = sem("w_out")
        consts_in = sem("consts_in")
        bq_scaled = sem("bq_scaled")
        ones_set = sem("ones_set")
        x_in = [sem(f"x_in{i}") for i in range(2)]
        res_in = [sem(f"res_in{i}") for i in range(2)]
        wv_in = sem("wv_in")
        wqk_in = [sem(f"wqk_in{i}") for i in range(2)]
        t_out = [sem(f"t_out{i}") for i in range(2)]
        n2_out = sem("n2_out")
        aff_out = sem("aff_out")
        stats_done = [sem(f"stats_done{n}") for n in range(2)]
        mv_done = [sem(f"mv_done{n}") for n in range(2)]
        ve_done = [sem(f"ve_done{n}") for n in range(2)]
        std_done = [sem(f"std_done{n}") for n in range(2)]
        newton = [sem(f"newton{n}") for n in range(2)]
        norm_done = [sem(f"norm_done{n}") for n in range(2)]
        ring_filled = sem("ring_filled")
        ring_hi = sem("ring_hi")
        ring_lo = sem("ring_lo")
        v_filled = sem("v_filled")
        v_sum = sem("v_sum")
        v_hi = sem("v_hi")
        v_lo = sem("v_lo")
        xbo = sem("xbo")
        s_filled = sem("s_filled")
        max_done = sem("max_done")
        exp_done = sem("exp_done")
        rinv_done = sem("rinv_done")
        rbc_done = sem("rbc_done")
        pv_done = sem("pv_done")
        o_copied = sem("o_copied")
        o_sum = sem("o_sum")
        o_norm = sem("o_norm")
        os_hi = sem("os_hi")
        os_lo = sem("os_lo")
        y_filled = sem("y_filled")
        t_done = sem("t_done")
        n2_filled = sem("n2_filled")
        n2_copied = sem("n2_copied")
        logits = sem("logits")
        soft = sem("soft")
        soft_exp = sem("soft_exp")
        affT_filled = sem("affT_filled")
        affT_copied = sem("affT_copied")
        sp_passed, pool_passed, dve_passed = sem("sp_passed"), sem("pool_passed"), sem("dve_passed")

        block = ctx.enter_context(nc.Block())

        def all_images(engine, image):
            with engine.Fori(0, B - 1) as b:
                image(b, False)
            image(B - 1, True)

        EARLY = 2 * (PAIRS - 1)
        QB = NT // 2
        PIECES = EARLY + QB

        def piece(j):
            if j < EARLY:
                return j // 2, slice(j % 2 * 512, j % 2 * 512 + 512)
            return PAIRS - 1, slice((j - EARLY) * QC, (j - EARLY) * QC + QC)

        def blocks_of_piece(j):
            if j < EARLY:
                return j // 2 * NT + QB + 2 * (j % 2) + 2
            return BLOCKS - QB + (j - EARLY) + 1

        @block.sync
        def _(sp):
            def load_x(j):
                for i in range(2):
                    sp.dma_start(xt[:, 4 * i:4 * i + 4, :],
                                 x[j, :, :].rearrange("(i p) c -> p i c", p=P)[:, 4 * i:4 * i + 4, :]
                                 ).then_inc(x_in[i], 16)

            def load_pair(p):
                sp.dma_start(wqk[:, p % 2, :, :, :].bitcast(F32), wqk_dram[p]).then_inc(wqk_in[p % 2], 16)

            load_x(0)
            raw = prob[:, :, :].rearrange("p a n -> p (a n)").rearrange("p (k c) -> p k c", k=KC)
            sp.dma_start(raw, wT[2]).then_inc(wv_raw_in, 16)
            for j in range(2):
                raw = oT[:, 2 * j:2 * j + 2, :].rearrange("p a n -> p (a n)").rearrange("p (k c) -> p k c", k=KC)
                sp.dma_start(raw, wT[j]).then_inc(wqk_raw_in, 16)
            sp.dma_start(bqk[:, :, :], b_col).then_inc(consts_in, 16)
            sp.dma_start(bv_bc[:, :], b_row[2:3, :].broadcast_to([P, C])).then_inc(consts_in, 16)
            sp.dma_start(bo_bc[:, :], b_row[3:4, :].broadcast_to([P, C])).then_inc(consts_in, 16)
            sp.dma_start(gate_sb[:, :, :], gate).then_inc(consts_in, 16)
            sp.wait_ge(w_lo, 1)
            sp.dma_start(wv_dram, wv.bitcast(F32)).then_inc(wv_out, 16)
            sp.wait_ge(w_lo, 3)
            for p in range(PAIRS):
                for j in range(2):
                    for h in range(2):
                        half = PT[:, h, j, :, :].rearrange("p t q -> p (t q)").bitcast(F32).rearrange(
                            "p (k c) -> p k c", k=KC)
                        sp.dma_start(wqk_dram[p, :, 2 * j + h, :, :],
                                     half[:, :, p * P:(p + 1) * P]).then_inc(w_out if p else w0_out, 16)
            raw = oT[:, 0:2, :].rearrange("p a n -> p (a n)").rearrange("p (k c) -> p k c", k=KC)
            sp.dma_start(raw, wT[3]).then_inc(wo_raw_in, 16)
            sp.wait_ge(v_filled, NT)
            sp.wait_ge(wv_out, 16)
            sp.wait_ge(w0_out, 16 * 4)
            load_pair(0)
            sp.wait_ge(w_out, 16 * 4 * (PAIRS - 1))
            load_pair(1)

            def image(b, last):
                if not last:
                    sp.wait_ge(ring_filled, b * RING + ring_norm(NT - 1) + 1)
                    load_x(b + 1)
                for p in range(2, PAIRS):
                    sp.wait_ge(ring_filled, b * RING + ring_proj(p - 2, 3) + 1)
                    load_pair(p)
                if not last:
                    sp.wait_ge(ring_filled, b * RING + ring_proj(PAIRS - 1, 3) + 1)
                    sp.dma_start(wv.bitcast(F32), wv_dram).then_inc(wv_in, 16)
                src = x[b, :, :].rearrange("(i p) c -> p i c", p=P)
                dst = oT[:, 0:3, :].rearrange("p k (h c) -> p k h c", c=C)
                sp.wait_ge(os_lo, b * PIECES + EARLY)
                for k in range(2):
                    sp.dma_start(dst[:, k, :, :], src[:, 2 * k:2 * k + 2, :]).then_inc(res_in[0], 16)
                sp.dma_start(dst[:, 2, :, :], src[:, 4:6, :]).then_inc(res_in[1], 16)
                sp.dma_start(spare[:, :, :], src[:, 6:8, :]).then_inc(res_in[1], 16)
                rows = out[b, :, :].rearrange("(i p) c -> i p c", p=P)
                n2_rows = n2_dram[b, :, :].rearrange("(i p) c -> i p c", p=P)
                for i in range(NT):
                    sp.wait_ge(t_done, b * NT + i + 1)
                    sp.dma_start(rows[i, :, :], res(i)).then_inc(t_out[i // 4], 16)
                for i in range(NT):
                    sp.wait_ge(norm_done[1], b * NT + i + 1)
                    sp.dma_start(n2_rows[i, :, :], res(i)).then_inc(n2_out, 16)
                if not last:
                    sp.wait_ge(v_filled, b * NT + 2 * NT)
                    load_pair(0)
                    load_pair(1)
                sp.wait_ge(affT_copied, b * 2 + 2)
                sp.dma_start(aff_dram[b, :, :], affT).then_inc(aff_out, 16)
                sp.wait_ge(t_out[0], b * (16 * 4) + 16 * 4)
                sp.wait_ge(t_out[1], b * (16 * 4) + 16 * 4)
                sp.wait_ge(n2_out, b * (16 * NT) + 16 * NT)
                sp.wait_ge(aff_out, b * 16 + 16)
                sp.sem_inc(sp_passed, 1)

            all_images(sp, image)

        @block.gpsimd
        def _(pool):
            def low_of_v(j):
                for i in range(NT):
                    pool.wait_ge(v_hi, j * NT + i + 1)
                    src = tok[:, i % 4, :].rearrange("p (a h d) -> p a h d", a=PAIRS, h=2)
                    nc.gpsimd.tensor_tensor(V[:, i, :, 1:3, :], src,
                                            V[:, i, :, 0:4:3, :].bitcast(F32), ALU.subtract).then_inc(v_lo, 1)

            nc.gpsimd.memset(ones[:, :], 1.0).then_inc(ones_set, 1)
            pool.wait_ge(ones_set, 1)
            pool.wait_ge(consts_in, 64)
            low_of_v(0)

            def image(b, last):
                def low_of_output(j, blocks):
                    chunk, cols = piece(j)
                    pool.wait_ge(o_norm, b * BLOCKS + blocks)
                    pool.wait_ge(os_hi, b * PIECES + j + 1)
                    nc.gpsimd.tensor_tensor(oS[:, 1, chunk, cols], oT[:, chunk, cols],
                                            oS[:, 0, chunk, cols].bitcast(F32), ALU.subtract).then_inc(os_lo, 1)

                def add_bo(i):
                    if i % 4 == 0:
                        pool.wait_ge(res_in[i // 4], b * 32 + 32)
                    nc.gpsimd.tensor_tensor(res(i), res(i), bo_bc[:, :], ALU.add).then_inc(xbo, 1)

                for k in range(BLOCKS + 2):
                    if k < BLOCKS:
                        if k >= 3:
                            pool.wait_ge(o_norm, b * BLOCKS + k - 2)
                        pool.wait_ge(rinv_done, b * BLOCKS + k + 1)
                        if k >= 2:
                            pool.wait_ge(pv_done, b * BLOCKS + k - 1)
                        pool.sem_inc(pool_passed, 1)
                        for j in range(2):
                            last_bc = nc.gpsimd.tensor_scalar(rinv_bc[:, k % 2, j, :], ones[:, :],
                                                              rinv[:, 2 * k + j:2 * k + j + 1], None, ALU.mult)
                        last_bc.then_inc(rbc_done, 1)
                    if k >= 2:
                        m = k - 2
                        pair, odd, q = m // NT, m // QB % 2, m % QB
                        rows = slice(D * odd, D * odd + D)
                        if k < BLOCKS:
                            pool.wait_ge(rbc_done, b * BLOCKS + k + 1)
                        elif k == BLOCKS:
                            pool.wait_ge(xbo, b * NT + 4)
                        else:
                            pool.wait_ge(os_lo, b * PIECES + PIECES - 1)
                        pool.wait_ge(o_sum, b * BLOCKS + m + 1)
                        nc.gpsimd.tensor_tensor(oT[rows, pair, q * QC:(q + 1) * QC], oSum[rows, m % 2, :],
                                                Rs[rows, m % 2, :], ALU.mult).then_inc(o_norm, 1)
                        if 3 * NT <= k < 3 * NT + 3:
                            for j in range(2):
                                low_of_output(2 * (k - 3 * NT) + j, m + 1)
                        if m >= BLOCKS - QB:
                            low_of_output(EARLY + m - (BLOCKS - QB), m + 1)
                        if BLOCKS - 2 <= k < BLOCKS:
                            for i in range(2):
                                add_bo(2 * (k - BLOCKS + 2) + i)
                for i in range(4, NT):
                    add_bo(i)
                if not last:
                    low_of_v(b + 1)
                pool.wait_ge(n2_out, b * (16 * NT) + 16 * NT)
                pool.wait_ge(aff_out, b * 16 + 16)
                pool.sem_inc(pool_passed, 1)

            all_images(pool, image)

        @block.scalar
        def _(act):
            def root(n, count, tiles):
                act.wait_ge(ve_done[n], count + 1)
                nc.scalar.activation(std[:, n, tiles], ve[:, n, tiles], ACT.Sqrt).then_inc(std_done[n], 1)

            def high_of_norm(j, i):
                k = ring_norm(i)
                act.wait_ge(ring_filled, j * RING + k + 1)
                nc.scalar.activation(nT[:, 0, :, i * P:(i + 1) * P],
                                     ring[:, k % 2, :].rearrange("p (k t) -> p k t", k=KC),
                                     ACT.Copy).then_inc(ring_hi, 1)

            def high_of_v(j, i):
                act.wait_ge(v_sum, j * NT + i + 1)
                src = tok[:, i % 4, :].rearrange("p (a h d) -> p a h d", a=PAIRS, h=2)
                nc.scalar.activation(V[:, i, :, 0:4:3, :], src, ACT.Copy).then_inc(v_hi, 1)

            def high_of_proj(j, p):
                for r in range(4):
                    k = ring_proj(p, r)
                    act.wait_ge(ring_filled, j * RING + k + 1)
                    nc.scalar.activation(qk[:, r // 2, 0, (r % 2) * 512:(r % 2) * 512 + 512],
                                         ring[:, k % 2, :], ACT.Identity,
                                         bias=bqk[:, r // 2, p:p + 1]).then_inc(ring_hi, 1)

            root(0, 0, slice(0, NT))
            for i in range(NT):
                if i == 0:
                    act.wait_ge(w_lo, 1)
                high_of_norm(0, i)
            for i in range(NT):
                high_of_v(0, i)
            act.wait_ge(bq_scaled, 1)
            high_of_proj(0, 0)

            def image(b, last):
                def high_of_output(j):
                    chunk, cols = piece(j)
                    act.wait_ge(o_norm, b * BLOCKS + blocks_of_piece(j))
                    nc.scalar.activation(oS[:, 0, chunk, cols], oT[:, chunk, cols], ACT.Copy).then_inc(os_hi, 1)

                for s in range(UNITS + 5):
                    if 0 < s < UNITS and s % UP == 0:
                        high_of_proj(b, s // UP)
                    if s == UNITS:
                        high_of_output(EARLY)
                    if 1 <= s <= UNITS:
                        u = s - 1
                        for c in range(2):
                            k = ring_probs(u, c)
                            act.wait_ge(ring_filled, b * RING + k + 1)
                            if u // 2 >= 2 and u % 2 == 0 and c == 0:
                                act.wait_ge(pv_done, b * BLOCKS + u // 2 - 1)
                            nc.scalar.activation(PT[:, 0, u // 2 % 2, 4 * c:4 * c + 4, u % 2 * P:u % 2 * P + P],
                                                 ring[:, k % 2, :].rearrange("p (m q) -> p m q", m=4),
                                                 ACT.Copy).then_inc(ring_hi, 1)
                    if s < UNITS:
                        if s == 0:
                            act.wait_ge(v_lo, b * NT + NT)
                        if s >= 2:
                            act.wait_ge(ring_filled, b * RING + ring_probs(s - 2, 1) + 1)
                        act.wait_ge(max_done, b * UNITS + s + 1)
                        nc.scalar.activation(prob[:, s % 2, :], S[:, s % 2, :], ACT.Exp, bias=nmax[:, s:s + 1],
                                             accum_out=rsum[:, s:s + 1]).then_inc(exp_done, 1)
                    if s >= 5 and s % 2 == 1:
                        m = (s - 5) // 2
                        odd = m // QB % 2
                        rows, other = slice(D * odd, D * odd + D), slice(D * (1 - odd), D * (1 - odd) + D)
                        act.wait_ge(pv_done, b * BLOCKS + m + 1)
                        if m >= 2:
                            act.wait_ge(o_norm, b * BLOCKS + m - 1)
                        nc.scalar.activation(Rs[rows, m % 2, :], O[rows, m % 2, QC:2 * QC], ACT.Copy)
                        nc.scalar.activation(oL[rows, m % 2, :], O[other, m % 2, 0:QC], ACT.Copy
                                             ).then_inc(o_copied, 1)
                    if s in EARLY_AT:
                        high_of_output(EARLY_AT.index(s))
                    if s == UNITS - 1 and not last:
                        root(0, b + 1, slice(0, NT))
                    if s == UNITS + 1:
                        high_of_output(EARLY + 1)
                    if s == UNITS + 3:
                        high_of_output(EARLY + 2)
                        high_of_output(EARLY + 3)
                for kind, i in WRAP:
                    if kind == "root":
                        root(1, b * 2 + i, slice(4 * i, 4 * i + 4))
                    if kind == "norm" and not last:
                        high_of_norm(b + 1, i)
                    if kind == "v" and not last:
                        high_of_v(b + 1, i)
                for i in range(NT):
                    act.wait_ge(n2_filled, b * NT + i + 1)
                    nc.scalar.activation(n2T[:, i % 2, :, :], S4[:, i % 4, :].rearrange("p (k t) -> p k t", k=KC),
                                         ACT.Copy).then_inc(n2_copied, 1)
                act.wait_ge(soft, b * 5 + 2)
                nc.scalar.activation(lg[:, :, :], lg[:, :, :], ACT.Exp).then_inc(soft_exp, 1)
                if not last:
                    high_of_proj(b + 1, 0)
                for i in range(2):
                    act.wait_ge(affT_filled, b * 2 + i + 1)
                    nc.scalar.activation(affT[:, 512 * i:512 * i + 512], O[0:E, 1 - i, :], ACT.Copy
                                         ).then_inc(affT_copied, 1)

            all_images(act, image)

        @block.vector
        def _(dve):
            def split(w, raw, hi, lo, scale=1.0):
                nc.vector.tensor_scalar(hi, raw, scale, None, ALU.mult).then_inc(w_hi, 1)
                dve.wait_ge(w_hi, w + 1)
                nc.vector.scalar_tensor_tensor(out=lo, in0=raw, scalar=scale, in1=hi.bitcast(F32),
                                               op0=ALU.mult, op1=ALU.subtract).then_inc(w_lo, 1)

            def flat(ap):
                return ap.rearrange("p a n -> p (a n)")

            def statistics(n, j, i, src):
                nc.vector.bn_stats(stats[:, n, i, :], src).then_inc(stats_done[n], 1)

            def variance(n, count, tiles, done, eps):
                dve.wait_ge(stats_done[n], done)
                dve.sem_inc(dve_passed, 1)
                for i in range(tiles.start, tiles.stop):
                    last_mv = nc.vector.bn_aggr(mv[:, n, i, :], stats[:, n, i, :])
                last_mv.then_inc(mv_done[n], 1)
                dve.wait_ge(mv_done[n], count + 1)
                nc.vector.tensor_scalar(ve[:, n, tiles], mv[:, n, tiles, 1], eps, None, ALU.add
                                        ).then_inc(ve_done[n], 1)

            def inverse_root(n, count, tiles):
                a, c, out_r, v_e = r0[:, tiles], r1[:, tiles], rstd[:, n, tiles], ve[:, n, tiles]
                dve.wait_ge(std_done[n], count + 1)
                nc.vector.reciprocal(a, std[:, n, tiles]).then_inc(newton[n], 1)
                dve.wait_ge(newton[n], count * 5 + 1)
                nc.vector.tensor_tensor(c, a, a, ALU.mult).then_inc(newton[n], 1)
                dve.wait_ge(newton[n], count * 5 + 2)
                nc.vector.tensor_tensor(out_r, c, v_e, ALU.mult).then_inc(newton[n], 1)
                dve.wait_ge(newton[n], count * 5 + 3)
                nc.vector.tensor_scalar(c, out_r, -0.5, 1.5, ALU.mult, ALU.add).then_inc(newton[n], 1)
                dve.wait_ge(newton[n], count * 5 + 4)
                nc.vector.tensor_tensor(out_r, a, c, ALU.mult).then_inc(newton[n], 1)
                dve.wait_ge(newton[n], count * 5 + 5)

            def normalise(n, i, tile):
                nc.vector.tensor_scalar(tile, tile, mv[:, n, i, 0:1], rstd[:, n, i:i + 1],
                                        ALU.subtract, ALU.mult).then_inc(norm_done[n], 1)

            def low_of_norm(j, i):
                k = ring_norm(i)
                dve.wait_ge(ring_hi, j * RING + k + 1)
                nc.vector.tensor_tensor(nT[:, 1, :, i * P:(i + 1) * P],
                                        ring[:, k % 2, :].rearrange("p (k t) -> p k t", k=KC),
                                        nT[:, 0, :, i * P:(i + 1) * P].bitcast(F32),
                                        ALU.subtract).then_inc(ring_lo, 1)

            def sum_of_v(j, i):
                dve.wait_ge(v_filled, j * NT + i + 1)
                if i >= 4:
                    dve.wait_ge(v_lo, j * NT + i - 3)
                nc.vector.tensor_tensor(tok[:, i % 4, :], O[:, i % 2, :], bv_bc[:, :], ALU.add).then_inc(v_sum, 1)

            def low_of_proj(j, p):
                for r in range(4):
                    k = ring_proj(p, r)
                    cols = slice((r % 2) * 512, (r % 2) * 512 + 512)
                    dve.wait_ge(ring_hi, j * RING + k + 1)
                    nc.vector.scalar_tensor_tensor(
                        out=qk[:, r // 2, 1, cols], in0=ring[:, k % 2, :], scalar=bqk[:, r // 2, p:p + 1],
                        in1=qk[:, r // 2, 0, cols].bitcast(F32), op0=ALU.add, op1=ALU.subtract
                    ).then_inc(ring_lo, 1)

            for i in range(NT):
                if i % 4 == 0:
                    dve.wait_ge(x_in[i // 4], 16)
                statistics(0, 0, i, xt[:, i, :])
            variance(0, 0, slice(0, NT), NT, EPS1)
            inverse_root(0, 0, slice(0, NT))
            for i in range(NT):
                normalise(0, i, xt[:, i, :])
            dve.wait_ge(wv_raw_in, 16)
            wv_flat = wqk[:, :, :, :, :].rearrange("p s w k c -> p s (w k c)")
            split(0, flat(prob[:, :, :]), wv_flat[:, 0, :], wv_flat[:, 1, :])
            for i in range(NT):
                low_of_norm(0, i)
            dve.wait_ge(wqk_raw_in, 32)
            for j in range(2):
                split(1 + j, flat(oT[:, 2 * j:2 * j + 2, :]), flat(PT[:, 0, j, :, :]), flat(PT[:, 1, j, :, :]),
                      D ** -0.5 if j == 0 else 1.0)
            dve.wait_ge(consts_in, 64)
            nc.vector.tensor_scalar(bqk[:, 0, :], bqk[:, 0, :], D ** -0.5, None, ALU.mult).then_inc(bq_scaled, 1)
            dve.wait_ge(bq_scaled, 1)
            for i in range(NT):
                sum_of_v(0, i)
            dve.wait_ge(wo_raw_in, 16)
            split(3, flat(oT[:, 0:2, :]), wo[:, 0, :, :].rearrange("p k c -> p (k c)"),
                  wo[:, 1, :, :].rearrange("p k c -> p (k c)"))
            low_of_proj(0, 0)

            def image(b, last):
                def tile_t(i):
                    dve.wait_ge(y_filled, b * NT + i + 1)
                    dve.wait_ge(xbo, b * NT + i + 1)
                    nc.vector.tensor_tensor(res(i), S4[:, i % 4, :], res(i), ALU.add).then_inc(t_done, 1)
                    dve.wait_ge(t_done, b * NT + i + 1)
                    statistics(1, b, i, res(i))

                def sum_of_o(m):
                    odd = m // QB % 2
                    rows = slice(D * odd, D * odd + D)
                    dve.wait_ge(o_copied, b * BLOCKS + m + 1)
                    nc.vector.tensor_tensor(oSum[rows, m % 2, :], O[rows, m % 2, 0:QC], oL[rows, m % 2, :],
                                            ALU.add).then_inc(o_sum, 1)

                for s in range(UNITS + 1):
                    if 0 < s < UNITS and s % UP == 0:
                        low_of_proj(b, s // UP)
                    if s < UNITS:
                        dve.wait_ge(s_filled, b * UNITS + s + 1)
                        nc.vector.tensor_reduce(nmax[:, s:s + 1], S[:, s % 2, :], AX.X, ALU.max, negate=True
                                                ).then_inc(max_done, 1)
                    if s >= 6 and s % 2 == 0:
                        sum_of_o((s - 6) // 2)
                    if s >= 1:
                        u = s - 1
                        for c in range(2):
                            k = ring_probs(u, c)
                            here = (u // 2 % 2, slice(4 * c, 4 * c + 4), slice(u % 2 * P, u % 2 * P + P))
                            dve.wait_ge(ring_hi, b * RING + k + 1)
                            nc.vector.tensor_tensor(PT[:, 1, here[0], here[1], here[2]],
                                                    ring[:, k % 2, :].rearrange("p (m q) -> p m q", m=4),
                                                    PT[:, 0, here[0], here[1], here[2]].bitcast(F32),
                                                    ALU.subtract).then_inc(ring_lo, 1)
                        if u % 2 == 1:
                            dve.wait_ge(exp_done, b * UNITS + u + 1)
                            nc.vector.reciprocal(rinv[:, u - 1:u + 1], rsum[:, u - 1:u + 1]).then_inc(rinv_done, 1)
                    if not last and 18 <= s < 18 + NT:
                        i = s - 18
                        if i % 4 == 0:
                            dve.wait_ge(x_in[i // 4], b * 16 + 32)
                        statistics(0, b + 1, i, xt[:, i, :])
                    if not last and s == 18 + NT:
                        variance(0, b + 1, slice(0, NT), b * NT + 2 * NT, EPS1)
                if not last:
                    inverse_root(0, b + 1, slice(0, NT))
                for i in range(NT):
                    if i == 1:
                        sum_of_o(BLOCKS - 2)
                        tile_t(0)
                        tile_t(1)
                    if i == 2:
                        sum_of_o(BLOCKS - 1)
                        tile_t(2)
                        tile_t(3)
                        variance(1, b * 2, slice(0, 4), b * NT + 4, EPS2)
                    if not last:
                        normalise(0, i, xt[:, i, :])
                for kind, i in WRAP:
                    if kind == "root":
                        inverse_root(1, b * 2 + i, slice(4 * i, 4 * i + 4))
                    if kind == "t":
                        tile_t(i)
                        if i == NT - 1:
                            variance(1, b * 2 + 1, slice(4, 8), b * NT + NT, EPS2)
                    if kind == "n2":
                        if i % 4 == 0:
                            dve.wait_ge(t_out[i // 4], b * 64 + 64)
                        normalise(1, i, res(i))
                    if kind == "norm" and not last:
                        low_of_norm(b + 1, i)
                    if kind == "v" and not last:
                        sum_of_v(b + 1, i)
                dve.wait_ge(logits, b * 1 + 1)
                lgp = O[:, 0, 0:NT * E].rearrange("p (i e) -> p i e", e=E)
                nc.vector.tensor_reduce(gmax[:, :], lgp, AX.X, ALU.max).then_inc(soft, 1)
                dve.wait_ge(soft, b * 5 + 1)
                nc.vector.tensor_tensor(lg[:, :, :], lgp, gmax[:, :].unsqueeze(2).broadcast_to([P, NT, E]),
                                        ALU.subtract).then_inc(soft, 1)
                dve.wait_ge(soft_exp, b * 1 + 1)
                nc.vector.tensor_reduce(gsum[:, :], lg[:, :, :], AX.X, ALU.add).then_inc(soft, 1)
                dve.wait_ge(soft, b * 5 + 3)
                nc.vector.reciprocal(grec[:, :], gsum[:, :]).then_inc(soft, 1)
                dve.wait_ge(soft, b * 5 + 4)
                nc.vector.tensor_tensor(aff[:, :, :], lg[:, :, :], grec[:, :].unsqueeze(2).broadcast_to([P, NT, E]),
                                        ALU.mult).then_inc(soft, 1)
                if not last:
                    low_of_proj(b + 1, 0)

            all_images(dve, image)

        @block.tensor
        def _(pe):
            def products(dst, pairs):
                for n, (l, r) in enumerate(pairs):
                    last_mm = nc.tensor.matmul(dst, l, r, start=(n == 0), stop=(n == len(pairs) - 1))
                return last_mm

            HL = [(0, 0), (0, 1), (1, 0)]

            def turn_norm(j, i, first):
                k = ring_norm(i)
                pe.wait_ge(norm_done[0], j * NT + i + 1)
                if not first or i >= 2:
                    pe.wait_ge(ring_lo, j * RING + k - 1)
                for c in range(KC):
                    last_t = nc.tensor.transpose(ring[:, k % 2, c * P:(c + 1) * P], xt[:, i, c * P:(c + 1) * P], ident)
                last_t.then_inc(ring_filled, 1)

            def project_v(j, i):
                pe.wait_ge(ring_lo, j * RING + ring_norm(i) + 1)
                if i >= 2:
                    pe.wait_ge(v_sum, j * NT + i - 1)
                products(O[:, i % 2, :], [(nT[:, l, c, i * P:(i + 1) * P], wv[:, w, c, :])
                                          for c in range(KC) for l, w in HL]).then_inc(v_filled, 1)

            def project_pair(j, p):
                pe.wait_ge(wqk_in[p % 2], j * 32 + 16 * (p // 2) + 16)
                for r in range(4):
                    k = ring_proj(p, r)
                    pe.wait_ge(ring_lo, j * RING + k - 1)
                    products(ring[:, k % 2, :],
                             [(wqk[:, p % 2, 2 * (r // 2) + w, c, :], nT[:, l, c, (r % 2) * 512:(r % 2) * 512 + 512])
                              for c in range(KC) for w, l in HL]).then_inc(ring_filled, 1)

            for i in range(NT):
                turn_norm(0, i, True)
            pe.wait_ge(w_lo, 1)
            for i in range(NT):
                project_v(0, i)
            project_pair(0, 0)
            pe.wait_ge(w_lo, 4)

            def image(b, last):
                def product_with_v(m, part):
                    head = m // QB
                    if part == 0:
                        if m == 0:
                            pe.wait_ge(v_lo, b * NT + NT)
                        if m >= 2:
                            pe.wait_ge(o_sum, b * BLOCKS + m - 1)
                        pe.wait_ge(ring_lo, b * RING + ring_probs(2 * m + 1, 1) + 1)
                    for t in range(4 * part, 4 * part + 4):
                        for l in range(2):
                            nc.tensor.matmul(
                                O[:, m % 2, 0:QC],
                                V[:, t, head // 2, 2 * (head % 2):2 * (head % 2) + 2, :].rearrange("p h d -> p (h d)"),
                                PT[:, l, m % 2, t, :],
                                start=(t + l == 0), stop=(t == NT - 1 and l == 1))
                    if part == 1:
                        pe.wait_ge(rbc_done, b * BLOCKS + m + 1)
                        for j in range(2):
                            last_t = nc.tensor.transpose(O[:, m % 2, QC + j * P:QC + (j + 1) * P],
                                                         rinv_bc[:, m % 2, j, :], ident)
                        last_t.then_inc(pv_done, 1)

                def turn_probs(u):
                    pe.wait_ge(exp_done, b * UNITS + u + 1)
                    for c in range(2):
                        k = ring_probs(u, c)
                        pe.wait_ge(ring_lo, b * RING + k - 1)
                        for m in range(4):
                            last_t = nc.tensor.transpose(ring[:, k % 2, m * P:(m + 1) * P],
                                                         prob[:, u % 2, (4 * c + m) * P:(4 * c + m + 1) * P], ident)
                        last_t.then_inc(ring_filled, 1)

                def project_out(i):
                    pe.wait_ge(os_lo, b * PIECES + EARLY + i // 2 + 1)
                    if i < 4:
                        pe.wait_ge(exp_done, b * UNITS + UNITS - 1 + i // 2)
                    else:
                        pe.wait_ge(t_done, b * NT + i - 3)
                    products(S4[:, i % 4, :], [(oS[:, l, c, i * P:(i + 1) * P], wo[:, w, c, :])
                                               for c in range(KC) for l, w in HL]).then_inc(y_filled, 1)

                for s in range(UNITS):
                    if s > 0 and s % UP == 0:
                        project_pair(b, s // UP)
                    if s % UP == 0:
                        pe.wait_ge(ring_lo, b * RING + ring_proj(s // UP, 3) + 1)
                    odd, i = s // NT % 2, s % NT
                    rows = slice(D * odd, D * odd + D)
                    if s >= 2:
                        pe.wait_ge(exp_done, b * UNITS + s - 1)
                    for l in range(2):
                        for m in range(2):
                            for r in range(2 - l):
                                last_mm = nc.tensor.matmul(S[:, s % 2, 512 * m:512 * m + 512],
                                                           qk[rows, 0, l, i * P:(i + 1) * P],
                                                           qk[rows, 1, r, 512 * m:512 * m + 512],
                                                           start=(l + r == 0), stop=(l == 1))
                    last_mm.then_inc(s_filled, 1)
                    if s >= 4:
                        product_with_v((s - 4) // 2, s % 2)
                    if s >= 1:
                        turn_probs(s - 1)
                product_with_v(BLOCKS - 2, 0)
                project_out(0)
                turn_probs(UNITS - 1)
                product_with_v(BLOCKS - 2, 1)
                project_out(1)
                product_with_v(BLOCKS - 1, 0)
                product_with_v(BLOCKS - 1, 1)
                project_out(2)
                project_out(3)
                for kind, i in WRAP:
                    if kind == "t":
                        project_out(i)
                    if kind == "norm" and not last:
                        turn_norm(b + 1, i, False)
                    if kind == "v" and not last:
                        if i == 0:
                            pe.wait_ge(wv_in, b * 16 + 16)
                            pe.wait_ge(o_sum, b * BLOCKS + BLOCKS)
                        project_v(b + 1, i)
                pe.wait_ge(t_done, b * NT + NT)
                if last:
                    pe.wait_ge(o_sum, b * BLOCKS + BLOCKS)
                else:
                    pe.wait_ge(v_sum, b * NT + 2 * NT)
                for i in range(NT + 1):
                    if i < NT:
                        pe.wait_ge(norm_done[1], b * NT + i + 1)
                        if i >= 4:
                            pe.wait_ge(n2_copied, b * NT + i - 3)
                        for c in range(KC):
                            last_t = nc.tensor.transpose(S4[:, i % 4, c * P:(c + 1) * P],
                                                         res(i)[:, c * P:(c + 1) * P], ident)
                        last_t.then_inc(n2_filled, 1)
                    if i >= 1:
                        pe.wait_ge(n2_copied, b * NT + i)
                        last_mm = products(O[:, 0, (i - 1) * E:i * E],
                                           [(n2T[:, (i - 1) % 2, c, :], gate_sb[:, c, :]) for c in range(KC)])
                last_mm.then_inc(logits, 1)
                if not last:
                    project_pair(b + 1, 0)
                pe.wait_ge(soft, b * 5 + 5)
                for h in range(2):
                    for i in range(4):
                        last_t = nc.tensor.transpose(O[0:E, 1 - h, i * P:(i + 1) * P], aff[:, 4 * h + i, :], ident)
                    last_t.then_inc(affT_filled, 1)

            all_images(pe, image)


def program(nc, out, x, wT, b_row, b_col, gate, w1, w2, b1, b2):
    n2 = nc.dram_tensor("n2_rows", [B, N, C], F32).ap()
    aff = nc.dram_tensor("affinities", [B, E, N], F32).ap()
    with ExitStack() as ctx:
        ident = ctx.enter_context(nc.sbuf_tensor("ident", [P, P], F32))
        idx = ctx.enter_context(nc.sbuf_tensor("idx", [P, E * B], U32))
        gates = ctx.enter_context(nc.sbuf_tensor("gates", [P, E * B], F32))
        ident_made = ctx.enter_context(nc.semaphore("ident_made"))
        with nc.Block() as block:
            @block.gpsimd
            def _(pool):
                nc.gpsimd.memset(ident[:, :], 0.0).then_inc(ident_made, 1)
                pool.wait_ge(ident_made, 1)
                nc.gpsimd.affine_select(out=ident[:, :], in_=ident[:, :], compare_op=ALU.not_equal, fill=1.0,
                                        base=0, pattern=[[-1, P]], channel_multiplier=1).then_inc(ident_made, 1)
                pool.wait_ge(ident_made, 2)
        attention(nc, x, wT, b_row, b_col, gate, out, n2, aff, ident[:, :])
        choose_tokens(nc, aff, ident[:, :], idx[:, :], gates[:, :])
        experts(nc, w1, w2, b1, b2, out.rearrange("b n c -> (b n) c"), n2.rearrange("b n c -> (b n) c"),
                ident[:, :], idx[:, :], gates[:, :])


def choose_tokens(nc, aff_dram, ident, idx, gates):
    with ExitStack() as ctx:
        def sb(name, shape, dt=F32):
            return ctx.enter_context(nc.sbuf_tensor(name, shape, dt))

        def sem(name):
            return ctx.enter_context(nc.semaphore(name))

        work = sb("work", [P, 2, N])
        top8 = sb("top8", [P, CAP])
        pos = sb("pos", [P, CAP], U32)
        posf = sb("posf", [P, CAP])
        rowf = sb("rowf", [P, CAP])
        base_i = sb("base_i", [P, B, E], mybir.dt.int32)
        base_f = sb("base_f", [P, B, E])
        pt = ctx.enter_context(nc.psum_tensor("pt", [P, 2, 512], F32))
        aff_in = sem("aff_in")
        base_made = sem("base_made")
        picked = sem("picked")
        rows_made = sem("rows_made")
        turned = sem("turned")
        copied = sem("copied")
        block = ctx.enter_context(nc.Block())
        STEPS = CAP // 8

        @block.sync
        def _(sp):
            sp.dma_start(work[:, 0, :], aff_dram.rearrange("b e n -> (b e) n")).then_inc(aff_in, 16)

        @block.gpsimd
        def _(pool):
            nc.gpsimd.iota(base_i[:, :, :], pattern=[[N, B], [0, E]], base=0, channel_multiplier=0
                           ).then_inc(base_made, 1)

        @block.vector
        def _(dve):
            dve.wait_ge(aff_in, 16)
            for r in range(STEPS):
                src, dst = work[:, r % 2, :], work[:, 1 - r % 2, :]
                best = top8[:, 8 * r:8 * r + 8]
                nc.vector.max(best, src).then_inc(picked, 1)
                dve.wait_ge(picked, 2 * r + 1)
                nc.vector.max_index(pos[:, 8 * r:8 * r + 8], best, src)
                nc.vector.match_replace(dst, best, src, -1.0).then_inc(picked, 1)
                dve.wait_ge(picked, 2 * r + 2)
            nc.vector.tensor_copy(posf[:, :], pos[:, :]).then_inc(rows_made, 1)
            dve.wait_ge(base_made, 1)
            nc.vector.tensor_copy(base_f[:, :, :], base_i[:, :, :]).then_inc(rows_made, 1)
            dve.wait_ge(rows_made, 2)
            dve.wait_ge(turned, 1)
            nc.vector.tensor_tensor(idx.rearrange("p (e b) -> p b e", e=E),
                                    pt[:, 0, 0:P].rearrange("p (b e) -> p b e", e=E), base_f[:, :, :],
                                    ALU.add).then_inc(copied, 1)
            dve.wait_ge(turned, 2)
            nc.vector.tensor_copy(gates.rearrange("p (e b) -> p b e", e=E),
                                  pt[:, 1, 0:P].rearrange("p (b e) -> p b e", e=E)).then_inc(copied, 1)
            dve.wait_ge(copied, 2)

        @block.tensor
        def _(pe):
            pe.wait_ge(rows_made, 1)
            nc.tensor.transpose(pt[:, 0, 0:P], posf[:, :], ident).then_inc(turned, 1)
            nc.tensor.transpose(pt[:, 1, 0:P], top8[:, :], ident).then_inc(turned, 1)


def experts(nc, w1, w2, b1, b2, out_rows, n2_rows, ident, idx, gates):
    G = 4
    COLS = G * CAP
    with ExitStack() as ctx:
        def sb(name, shape, dt=F32):
            return ctx.enter_context(nc.sbuf_tensor(name, shape, dt))

        def sem(name):
            return ctx.enter_context(nc.semaphore(name))

        wraw = sb("wraw", [P, 2 * KC, FF])
        ws = sb("ws", [P, 2, 2, 2 * KC, FF], F32R)
        b1s = sb("b1s", [P, 2, KC])
        b2s = sb("b2s", [P, 2, C])
        idxc = sb("idxc", [P, 2, B], U32)
        gatec = sb("gatec", [P, 2, B])
        xg = sb("xg", [P, 2, G, C])
        xT = sb("xT", [P, 2, 2, KC, COLS], F32R)
        hf = sb("hf", [P, 2, COLS])
        hT = sb("hT", [P, 2, KC, COLS], F32R)
        y0 = sb("y0", [P, 2, C])
        y = sb("y", [P, 2, G, C])
        xr = ctx.enter_context(nc.psum_tensor("xr", [P, 2, 512], F32))
        p1 = ctx.enter_context(nc.psum_tensor("p1", [P, 2, 512], F32))
        p2 = ctx.enter_context(nc.psum_tensor("p2", [P, 4, 512], F32))

        w_in = sem("w_in")
        b12_in = [sem(f"b12_in{i}") for i in range(2)]
        ws_hi = sem("ws_hi")
        ws_lo = sem("ws_lo")
        cols_made = sem("cols_made")
        gathered = [sem(f"gathered{i}") for i in range(2)]
        xr_filled = sem("xr_filled")
        xr_hi = sem("xr_hi")
        xr_lo = sem("xr_lo")
        p1_filled = sem("p1_filled")
        h_done = sem("h_done")
        h_hi = sem("h_hi")
        h_lo = sem("h_lo")
        p2_filled = sem("p2_filled")
        y0_done = sem("y0_done")
        y_done = sem("y_done")
        added = [sem(f"added{i}") for i in range(B)]
        sp_passed2, pool_passed2 = sem("sp_passed2"), sem("pool_passed2")
        block = ctx.enter_context(nc.Block())
        WCH = 2 * KC

        def every_expert(engine, expert):
            expert(0, 0, False)
            expert(1, 1, False)
            with engine.Fori(1, E // 2 - 1) as twos:
                expert(2 * twos, 0, False)
                expert(2 * twos + 1, 1, False)
            expert(E - 2, 0, False)
            expert(E - 1, 1, True)

        def started(e, g, n):
            return type(e) is not int or e > 0 or g > 0 or n >= 0

        @block.sync
        def _(sp):
            def load(e, k):
                sp.dma_start(wraw[:, 0:KC, :], w1[e]).then_inc(w_in, 16)
                sp.dma_start(wraw[:, KC:2 * KC, :], w2[e]).then_inc(w_in, 16)
                sp.dma_start(b1s[:, k, :], b1[e]).then_inc(b12_in[k], 16)
                sp.dma_start(b2s[:, k, :], b2[e].broadcast_to([P, C])).then_inc(b12_in[k], 16)

            load(0, 0)
            sp.wait_ge(ws_lo, WCH)
            load(1, 1)
            with sp.Fori(0, E // 2 - 1) as twos:
                for k in range(2):
                    e = 2 * twos
                    sp.wait_ge(ws_lo, (e + k) * WCH + 2 * WCH)
                    sp.sem_inc(sp_passed2, 1)
                    sp.wait_ge(y0_done, (e + k) * (2 * G) + 2 * G)
                    load(e + k + 2, k)

        @block.gpsimd
        def _(pool):
            def columns(e, k):
                nc.gpsimd.tensor_copy(idxc[:, k, :], idx[:, bass.ds(e * B, B)])
                nc.gpsimd.tensor_copy(gatec[:, k, :], gates[:, bass.ds(e * B, B)]).then_inc(cols_made, 1)

            def gather(k, g):
                for j in range(G):
                    pool.indirect_dma_start(
                        out=xg[:, g, j, :], out_offset=None, in_=n2_rows,
                        in_offset=bass.IndirectOffsetOnAxis(ap=idxc[:, k, G * g + j:G * g + j + 1], axis=0),
                    ).then_inc(gathered[g], 16)

            def scatter(e, k, g):
                for j in range(G):
                    pool.wait_ge(y_done, e * (2 * G) + G * g + j + 1)
                    if type(e) is not int or e > 0:
                        pool.wait_ge(added[G * g + j], e * 16)
                    pool.sem_inc(pool_passed2, 1)
                    pool.indirect_dma_start(
                        out=out_rows, out_offset=bass.IndirectOffsetOnAxis(ap=idxc[:, k, G * g + j:G * g + j + 1], axis=0),
                        in_=y[:, g, j, :], in_offset=None, compute_op=ALU.add,
                    ).then_inc(added[G * g + j], 16)

            def expert(e, k, last):
                if not last:
                    if type(e) is not int or e > 0:
                        pool.wait_ge(y_done, e * (2 * G))
                        for i in range(B):
                            pool.wait_ge(added[i], e * 16)
                    columns(e + 1, 1 - k)
                    pool.wait_ge(cols_made, e + 2)
                for g in range(2):
                    if not last:
                        pool.wait_ge(xr_filled, e * (2 * G) + G * g + G)
                        pool.sem_inc(pool_passed2, 1)
                        gather(1 - k, g)
                    scatter(e, k, g)

            columns(0, 0)
            pool.wait_ge(cols_made, 1)
            gather(0, 0)
            gather(0, 1)
            every_expert(pool, expert)
            for i in range(B):
                pool.wait_ge(added[i], 16 * E)

        @block.scalar
        def _(act):
            def turn(v, g):
                for j in range(G):
                    act.wait_ge(xr_filled, v * G + j + 1)
                    nc.scalar.activation(xT[:, g, 0, :, j * P:(j + 1) * P],
                                         xr[:, j % 2, :].rearrange("p (k t) -> p k t", k=KC),
                                         ACT.Copy).then_inc(xr_hi, 1)

            def expert(e, k, last):
                act.wait_ge(b12_in[k], (e - k) * 16 + 32)
                act.wait_ge(cols_made, e + 1)
                for g in range(2):
                    v = e * 2 + g
                    for m in range(KC):
                        act.wait_ge(p1_filled, v * KC + m + 1)
                        if started(e, g, m - 2):
                            act.wait_ge(h_lo, v * KC + m - 1)
                        nc.scalar.activation(hf[:, m % 2, :], p1[:, m % 2, :], ACT.Gelu_apprx_tanh,
                                             bias=b1s[:, k, m:m + 1]).then_inc(h_done, 1)
                    if not (last and g == 1):
                        turn(v + 1, 1 - g)
                    for j in range(G):
                        act.wait_ge(y0_done, v * G + j + 1)
                        if started(e, 0, -1):
                            act.wait_ge(added[G * g + j], e * 16)
                        nc.scalar.activation(y[:, g, j, :], y0[:, j % 2, :], ACT.Copy,
                                             scale=gatec[:, k, G * g + j:G * g + j + 1]).then_inc(y_done, 1)

            turn(0, 0)
            every_expert(act, expert)

        @block.vector
        def _(dve):
            def split_chunk(e, k, c):
                if c == 0:
                    dve.wait_ge(w_in, e * 32 + 32)
                nc.vector.tensor_copy(ws[:, k, 0, c, :], wraw[:, c, :]).then_inc(ws_hi, 1)
                dve.wait_ge(ws_hi, e * WCH + c + 1)
                nc.vector.tensor_tensor(ws[:, k, 1, c, :], wraw[:, c, :], ws[:, k, 0, c, :].bitcast(F32),
                                        ALU.subtract).then_inc(ws_lo, 1)

            def turn(v, g):
                for j in range(G):
                    dve.wait_ge(xr_hi, v * G + j + 1)
                    nc.vector.tensor_tensor(xT[:, g, 1, :, j * P:(j + 1) * P],
                                            xr[:, j % 2, :].rearrange("p (k t) -> p k t", k=KC),
                                            xT[:, g, 0, :, j * P:(j + 1) * P].bitcast(F32),
                                            ALU.subtract).then_inc(xr_lo, 1)

            def expert(e, k, last):
                dve.wait_ge(b12_in[k], (e - k) * 16 + 32)
                for g in range(2):
                    v = e * 2 + g
                    for m in range(KC):
                        dve.wait_ge(h_done, v * KC + m + 1)
                        if m == 0 and started(e, g, -1):
                            dve.wait_ge(p2_filled, v * G)
                        nc.vector.tensor_copy(hT[:, 0, m, :], hf[:, m % 2, :]).then_inc(h_hi, 1)
                        dve.wait_ge(h_hi, v * KC + m + 1)
                        nc.vector.tensor_tensor(hT[:, 1, m, :], hf[:, m % 2, :], hT[:, 0, m, :].bitcast(F32),
                                                ALU.subtract).then_inc(h_lo, 1)
                    if not (last and g == 1):
                        turn(v + 1, 1 - g)
                    for j in range(G):
                        dve.wait_ge(p2_filled, v * G + j + 1)
                        if started(e, g, j - 2):
                            dve.wait_ge(y_done, v * G + j - 1)
                        nc.vector.tensor_tensor(y0[:, j % 2, :], p2[:, j, :], b2s[:, k, :], ALU.add
                                                ).then_inc(y0_done, 1)
                    if not last:
                        for c in range(4 * g, 4 * g + 4):
                            split_chunk(e + 1, 1 - k, c)

            for c in range(WCH):
                split_chunk(0, 0, c)
            turn(0, 0)
            every_expert(dve, expert)

        @block.tensor
        def _(pe):
            HL = [(0, 0), (0, 1), (1, 0)]

            def products(dst, pairs):
                for n, (l, r) in enumerate(pairs):
                    last = nc.tensor.matmul(dst, l, r, start=(n == 0), stop=(n == len(pairs) - 1))
                return last

            def turn(e, v, g):
                pe.wait_ge(gathered[g], e * (16 * G) + 16 * G)
                for j in range(G):
                    if type(v) is not int or v > 0 or j >= 2:
                        pe.wait_ge(xr_lo, v * G + j - 1)
                    for c in range(KC):
                        last = nc.tensor.transpose(xr[:, j % 2, c * P:(c + 1) * P], xg[:, g, j, c * P:(c + 1) * P],
                                                   ident)
                    last.then_inc(xr_filled, 1)

            def expert(e, k, last):
                pe.wait_ge(ws_lo, e * WCH + WCH)
                for g in range(2):
                    v = e * 2 + g
                    pe.wait_ge(xr_lo, v * G + G)
                    for m in range(KC):
                        if started(e, g, m - 2):
                            pe.wait_ge(h_done, v * KC + m - 1)
                        products(p1[:, m % 2, :], [(ws[:, k, w, c, m * P:(m + 1) * P], xT[:, g, l, c, :])
                                                   for c in range(KC) for w, l in HL]).then_inc(p1_filled, 1)
                    if not (last and g == 1):
                        turn(e + g, v + 1, 1 - g)
                    for j in range(G):
                        if j == 0:
                            pe.wait_ge(h_lo, v * KC + KC)
                        if started(e, g, -1):
                            pe.wait_ge(y0_done, v * G + j - 3)
                        products(p2[:, j, :], [(hT[:, l, c, j * P:(j + 1) * P], ws[:, k, w, KC + c, :])
                                               for c in range(KC) for l, w in HL]).then_inc(p2_filled, 1)

            turn(0, 0, 0)
            every_expert(pe, expert)


_OUT = "out_dram"


def kernel(**inputs):
    import numpy as np
    import concourse.bacc as bacc
    from concourse.bass_utils import run_bass_kernel_spmd

    nc = bacc.Bacc("TRN2", target_bir_lowering=False, num_devices=1)
    a = {k: np.asarray(v) for k, v in inputs.items()}

    def chunks(w):
        return w.reshape(*w.shape[:-2], KC, P, w.shape[-1]).swapaxes(-3, -2)

    biases = [a["L0_conv_bq"], a["L0_conv_bk"], a["L0_conv_bv"], a["L0_conv_bo"]]
    arrays = {
        "x_dram": a["x"].reshape(B, C, N).transpose(0, 2, 1),
        "wT_dram": np.stack([chunks(a["L0_conv_" + n].T) for n in ("Wq", "Wk", "Wv", "Wo")]),
        "b_row_dram": np.stack(biases),
        "b_col_dram": np.stack([v.reshape(KC, P).T for v in biases[:2]], 1),
        "gate_dram": chunks(a["L0_ffn_gate_weight"]),
        "w1_dram": chunks(a["L0_ffn_w1"]),
        "w2_dram": chunks(a["L0_ffn_w2"]),
        "b1_dram": a["L0_ffn_b1"].reshape(E, KC, P).transpose(0, 2, 1),
        "b2_dram": a["L0_ffn_b2"].reshape(E, 1, C),
    }
    arrays = {k: np.ascontiguousarray(v) for k, v in arrays.items()}
    d = {k: nc.dram_tensor(k, v.shape, F32, kind="ExternalInput").ap() for k, v in arrays.items()}
    out = nc.dram_tensor(_OUT, (B, N, C), F32, kind="ExternalOutput").ap()
    program(nc, out, **{k.removesuffix("_dram"): v for k, v in d.items()})
    r = run_bass_kernel_spmd(nc, [arrays], core_ids=[0])
    return np.ascontiguousarray(r.results[0][_OUT].transpose(0, 2, 1)).reshape(B, C, 32, 32)
```

```python
from contextlib import ExitStack

import concourse.bass as bass
from concourse import mybir

F32 = mybir.dt.float32
F32R = mybir.dt.float32r
U32 = mybir.dt.uint32
ACT = mybir.ActivationFunctionType
ALU = mybir.AluOpType
AX = mybir.AxisListType

P = 128
B, C, N = 8, 512, 1024
NT = N // P
KC = C // P
H, D = 8, 64
PAIRS = H // 2
E, FF = 16, 512
CAP = N // E * 2
EPS1, EPS2 = 1e-6, 1e-5

UP = 2 * NT
UNITS = PAIRS * UP
BLOCKS = UNITS // 2
QC = 2 * P

RING = NT + PAIRS * 4 + 2 * UNITS


def ring_norm(i):
    return i


def ring_proj(p, r):
    return NT + 4 * p + (2 * (UP * p - 2) if p else 0) + r


def ring_probs(u, c):
    return NT + 4 * min(PAIRS, (u + 2) // UP + 1) + 2 * u + c


def split_weights_dram(nc):
    wqk = nc.dram_tensor("wqk_split", [PAIRS, P, 4, KC, P], F32).ap()
    wv = nc.dram_tensor("wv_split", [P, 2, KC, C], F32).ap()
    return wqk, wv


EARLY_AT = [50, 52, 54, 55, 57, 59]
EARLY_BLOCK = [24, 25, 26, 26, 27, 28]

WRAP = [("norm", 0), ("root", 0), ("t", 4), ("norm", 1), ("n2", 0), ("t", 5), ("norm", 2), ("n2", 1),
        ("t", 6), ("norm", 3), ("n2", 2), ("t", 7), ("norm", 4), ("n2", 3), ("v", 0), ("root", 1), ("norm", 5),
        ("v", 1), ("n2", 4), ("norm", 6), ("v", 2), ("n2", 5), ("norm", 7), ("v", 3), ("n2", 6), ("v", 4),
        ("n2", 7), ("v", 5), ("v", 6), ("v", 7)]


def attention(nc, x, wT, b_row, b_col, gate, out, n2_dram, aff_dram, ident):
    wqk_dram, wv_dram = split_weights_dram(nc)
    with ExitStack() as ctx:
        def sb(name, shape, dt=F32):
            return ctx.enter_context(nc.sbuf_tensor(name, shape, dt))

        def sem(name):
            return ctx.enter_context(nc.semaphore(name))

        wqk = sb("wqk", [P, 4, KC, P], F32R)
        wo = sb("wo", [P, 2, KC, C], F32R)
        xt = sb("xt", [P, NT, C])
        nT = sb("nT", [P, 2, KC, N], F32R)
        oS = nT
        qs = sb("qs", [P, 2, N], F32R)
        kd = sb("kd", [P, 2, 2, N], F32R)
        V = sb("V", [P, NT, PAIRS, 4, D], F32R)
        prob = sb("prob", [P, 2, N])
        tok = prob[:, :, :].rearrange("p a (s c) -> p (a s) c", c=C)
        PT = sb("PT", [P, 2, 2, NT, QC], F32R)
        w0 = PT[:, 0, 0, :, :].rearrange("p t q -> p (t q)").rearrange(
            "p (w k c) -> p w k c", w=4, k=KC)
        wv = PT[:, :, 1, :, :].rearrange("p h t q -> p h (t q)").rearrange(
            "p h (k c) -> p h k c", k=KC)
        oT = sb("oT", [P, KC, N])
        spare = sb("spare", [P, 2, C])

        def res(i):
            return oT[:, i // 2, (i % 2) * C:(i % 2) * C + C] if i < 6 else spare[:, i - 6, :]

        affT = oT[0:E, KC - 1, :]
        tmp = sb("tmp", [P, 3, 2, QC])
        Rs = tmp[:, 0, :, :]
        oL = tmp[:, 1, :, :]
        oH = tmp[:, 2, :, :]
        n2T = tmp[:, 0:2, :, :].rearrange("p a q c -> p a (q c)").rearrange(
            "p a (k t) -> p a k t", k=KC)
        bv_bc = sb("bv_bc", [P, C])
        bo_bc = sb("bo_bc", [P, C])
        bqk = sb("bqk", [P, 2, KC])
        gate_sb = sb("gate_sb", [P, KC, E])
        nmax = sb("nmax", [P, UNITS])
        rsum = sb("rsum", [P, UNITS])
        rinv = sb("rinv", [P, UNITS])
        ones = sb("ones", [P, P])
        rinv_bc = sb("rinv_bc", [P, 2, 2, P])
        stats = sb("stats", [P, 2, NT, 6])
        mv = sb("mv", [P, 2, NT, 2])
        ve = sb("ve", [P, 2, NT])
        std = sb("std", [P, 2, NT])
        r0 = sb("r0", [P, NT])
        r1 = sb("r1", [P, NT])
        rstd = sb("rstd", [P, 2, NT])
        lg = sb("lg", [P, NT, E])
        aff = sb("aff", [P, NT, E])
        gmax = sb("gmax", [P, NT])
        gsum = sb("gsum", [P, NT])
        grec = sb("grec", [P, NT])
        unused = sb("unused", [P, 1])

        S = ctx.enter_context(nc.psum_tensor("S", [P, 2, N], F32))
        ring = ctx.enter_context(nc.psum_tensor("ring", [P, 2, 512], F32))
        O = ctx.enter_context(nc.psum_tensor("O", [P, 2, 512], F32))
        S4 = S[:, :, :].rearrange("p a (h n) -> p (a h) n", h=2)

        wv_raw_in = sem("wv_raw_in")
        wqk_raw_in = sem("wqk_raw_in")
        wo_raw_in = sem("wo_raw_in")
        w_hi = sem("w_hi")
        w_lo = sem("w_lo")
        wv_out = sem("wv_out")
        w0_out = sem("w0_out")
        w_out = sem("w_out")
        consts_in = sem("consts_in")
        bq_scaled = sem("bq_scaled")
        ones_set = sem("ones_set")
        x_in = [sem(f"x_in{i}") for i in range(2)]
        res_in = [sem(f"res_in{i}") for i in range(2)]
        wv_in = sem("wv_in")
        w0_in = sem("w0_in")
        wqk_in = sem("wqk_in")
        k_dup = sem("k_dup")
        t_out = [sem(f"t_out{i}") for i in range(2)]
        n2_out = sem("n2_out")
        aff_out = sem("aff_out")
        stats_done = [sem(f"stats_done{n}") for n in range(2)]
        mv_done = [sem(f"mv_done{n}") for n in range(2)]
        ve_done = [sem(f"ve_done{n}") for n in range(2)]
        std_done = [sem(f"std_done{n}") for n in range(2)]
        newton = [sem(f"newton{n}") for n in range(2)]
        norm_done = [sem(f"norm_done{n}") for n in range(2)]
        ring_filled = sem("ring_filled")
        ring_hi = sem("ring_hi")
        even_hi = sem("even_hi")
        ring_lo = sem("ring_lo")
        v_filled = sem("v_filled")
        v_sum = sem("v_sum")
        v_hi = sem("v_hi")
        v_lo = sem("v_lo")
        xbo = sem("xbo")
        s_filled = sem("s_filled")
        max_done = sem("max_done")
        exp_done = sem("exp_done")
        rinv_done = sem("rinv_done")
        rbc_done = sem("rbc_done")
        pv_read = sem("pv_read")
        pv_done = sem("pv_done")
        o_copied = sem("o_copied")
        o_sum = sem("o_sum")
        o_norm = sem("o_norm")
        os_hi = sem("os_hi")
        os_lo = sem("os_lo")
        y_filled = sem("y_filled")
        t_done = sem("t_done")
        n2_filled = sem("n2_filled")
        n2_copied = sem("n2_copied")
        logits = sem("logits")
        logits_copied = sem("logits_copied")
        logits_turned = sem("logits_turned")
        soft = sem("soft")
        soft_exp = sem("soft_exp")
        affT_filled = sem("affT_filled")
        affT_copied = sem("affT_copied")
        sp_passed, pool_passed = sem("sp_passed"), sem("pool_passed")
        dve_passed, pe_passed = sem("dve_passed"), sem("pe_passed")

        block = ctx.enter_context(nc.Block())

        def all_images(engine, image):
            with engine.Fori(0, B - 1) as b:
                image(b, False)
            image(B - 1, True)

        EARLY = 2 * (PAIRS - 1)
        QB = NT // 2
        PIECES = EARLY + QB

        def piece(j):
            if j < EARLY:
                return j // 2, slice(j % 2 * 512, j % 2 * 512 + 512)
            return PAIRS - 1, slice((j - EARLY) * QC, (j - EARLY) * QC + QC)

        def blocks_of_piece(j):
            if j < EARLY:
                return j // 2 * NT + QB + 2 * (j % 2) + 2
            return BLOCKS - QB + (j - EARLY) + 1

        def staged(j, h):
            if j == 0:
                return kd[:, h, :, :].rearrange("p l n -> p (l n)")
            return qs[:, :, :].rearrange("p a n -> p (a n)") if h == 0 else wqk[:, :, :, :].rearrange(
                "p w k c -> p (w k c)")

        def flat(ap):
            return ap.rearrange("p a n -> p (a n)")

        splits = [(flat(prob[:, :, :]), flat(PT[:, 0, 1, :, :]), flat(PT[:, 1, 1, :, :]), 1.0),
                  (flat(oT[:, 0:2, :]), staged(0, 0), staged(0, 1), D ** -0.5),
                  (flat(oT[:, 2:4, :]), staged(1, 0), staged(1, 1), 1.0),
                  (flat(oT[:, 0:2, :]), flat(wo[:, 0, :, :]), flat(wo[:, 1, :, :]), 1.0)]

        @block.sync
        def _(sp):
            def load_x(j):
                for i in range(2):
                    sp.dma_start(xt[:, 4 * i:4 * i + 4, :],
                                 x[j, :, :].rearrange("(i p) c -> p i c", p=P)[:, 4 * i:4 * i + 4, :]
                                 ).then_inc(x_in[i], 16)

            def load_pair(p):
                sp.dma_start(wqk[:, :, :, :].bitcast(F32), wqk_dram[p]).then_inc(wqk_in, 16)

            def load_first_pair():
                sp.dma_start(w0.bitcast(F32), wqk_dram[0]).then_inc(w0_in, 16)

            def duplicate_k(j, p):
                for r in range(2):
                    sp.wait_ge(ring_lo, j * RING + ring_proj(p, r) + 1)
                    cols = slice(r * 512, r * 512 + 512)
                    for odd in range(2):
                        rows, other = slice(D * odd, D * odd + D), slice(D * (1 - odd), D * (1 - odd) + D)
                        sp.dma_start(kd[other, odd, :, cols].bitcast(F32),
                                     kd[rows, odd, :, cols].bitcast(F32)).then_inc(k_dup, 16)

            load_x(0)
            raw = prob[:, :, :].rearrange("p a n -> p (a n)").rearrange("p (k c) -> p k c", k=KC)
            sp.dma_start(raw, wT[2]).then_inc(wv_raw_in, 16)
            sp.dma_start(bqk[:, :, :], b_col).then_inc(consts_in, 16)
            sp.dma_start(bv_bc[:, :], b_row[2:3, :].broadcast_to([P, C])).then_inc(consts_in, 16)
            sp.dma_start(bo_bc[:, :], b_row[3:4, :].broadcast_to([P, C])).then_inc(consts_in, 16)
            sp.dma_start(gate_sb[:, :, :], gate).then_inc(consts_in, 16)
            for j in range(2):
                raw = oT[:, 2 * j:2 * j + 2, :].rearrange("p a n -> p (a n)").rearrange("p (k c) -> p k c", k=KC)
                sp.dma_start(raw, wT[j]).then_inc(wqk_raw_in, 16)
            sp.wait_ge(w_lo, 1)
            sp.dma_start(wv_dram, wv.bitcast(F32)).then_inc(wv_out, 16)
            sp.wait_ge(w_lo, 3)
            for p in range(PAIRS):
                if p == 1:
                    raw = oT[:, 0:2, :].rearrange("p a n -> p (a n)").rearrange("p (k c) -> p k c", k=KC)
                    sp.dma_start(raw, wT[3]).then_inc(wo_raw_in, 16)
                    sp.wait_ge(w0_out, 16 * 4)
                    load_first_pair()
                for j in range(2):
                    for h in range(2):
                        half = staged(j, h).bitcast(F32).rearrange("p (k c) -> p k c", k=KC)
                        sp.dma_start(wqk_dram[p, :, 2 * j + h, :, :],
                                     half[:, :, p * P:(p + 1) * P]).then_inc(w_out if p else w0_out, 16)
            sp.wait_ge(w_out, 16 * 4 * (PAIRS - 1))
            load_pair(1)
            duplicate_k(0, 0)

            def image(b, last):
                if not last:
                    sp.wait_ge(ring_filled, b * RING + ring_norm(NT - 1) + 1)
                    load_x(b + 1)
                for p in range(1, PAIRS):
                    duplicate_k(b, p)
                    if p < PAIRS - 1 or not last:
                        sp.wait_ge(ring_filled, b * RING + ring_proj(p, 3) + 1)
                        load_pair(p % (PAIRS - 1) + 1)
                src = x[b, :, :].rearrange("(i p) c -> p i c", p=P)
                dst = oT[:, 0:3, :].rearrange("p k (h c) -> p k h c", c=C)
                for k in range(2):
                    sp.wait_ge(os_lo, b * PIECES + 2 * k + 2)
                    sp.dma_start(dst[:, k, :, :], src[:, 2 * k:2 * k + 2, :]).then_inc(res_in[0], 16)
                sp.wait_ge(os_lo, b * PIECES + EARLY)
                sp.dma_start(dst[:, 2, :, :], src[:, 4:6, :]).then_inc(res_in[1], 16)
                sp.dma_start(spare[:, :, :], src[:, 6:8, :]).then_inc(res_in[1], 16)
                if not last:
                    sp.wait_ge(pv_done, b * BLOCKS + BLOCKS)
                    sp.dma_start(wv.bitcast(F32), wv_dram).then_inc(wv_in, 16)
                    load_first_pair()
                rows = out[b, :, :].rearrange("(i p) c -> i p c", p=P)
                n2_rows = n2_dram[b, :, :].rearrange("(i p) c -> i p c", p=P)
                for i in range(NT):
                    sp.wait_ge(t_done, b * NT + i + 1)
                    sp.dma_start(rows[i, :, :], res(i)).then_inc(t_out[i // 4], 16)
                for i in range(NT):
                    sp.wait_ge(norm_done[1], b * NT + i + 1)
                    sp.dma_start(n2_rows[i, :, :], res(i)).then_inc(n2_out, 16)
                if not last:
                    duplicate_k(b + 1, 0)
                sp.wait_ge(affT_copied, b * 2 + 2)
                sp.dma_start(aff_dram[b, :, :], affT).then_inc(aff_out, 16)
                sp.wait_ge(t_out[0], b * (16 * 4) + 16 * 4)
                sp.wait_ge(t_out[1], b * (16 * 4) + 16 * 4)
                sp.wait_ge(n2_out, b * (16 * NT) + 16 * NT)
                sp.wait_ge(aff_out, b * 16 + 16)
                sp.sem_inc(sp_passed, 1)

            all_images(sp, image)

        @block.gpsimd
        def _(pool):
            def low_of_v(j):
                for i in range(NT):
                    pool.wait_ge(v_hi, j * NT + i + 1)
                    src = tok[:, i % 4, :].rearrange("p (a h d) -> p a h d", a=PAIRS, h=2)
                    nc.gpsimd.tensor_tensor(V[:, i, :, 1:3, :], src,
                                            V[:, i, :, 0:4:3, :].bitcast(F32), ALU.subtract).then_inc(v_lo, 1)

            nc.gpsimd.memset(ones[:, :], 1.0).then_inc(ones_set, 1)
            pool.wait_ge(ones_set, 1)
            pool.wait_ge(consts_in, 64)
            low_of_v(0)

            def image(b, last):
                def low_of_output(j, blocks):
                    chunk, cols = piece(j)
                    pool.wait_ge(o_norm, b * BLOCKS + blocks)
                    pool.wait_ge(os_hi, b * PIECES + j + 1)
                    nc.gpsimd.tensor_tensor(oS[:, 1, chunk, cols], oT[:, chunk, cols],
                                            oS[:, 0, chunk, cols].bitcast(F32), ALU.subtract).then_inc(os_lo, 1)

                def add_bo(i):
                    if i % 4 == 0:
                        pool.wait_ge(res_in[i // 4], b * 32 + 32)
                    nc.gpsimd.tensor_tensor(res(i), res(i), bo_bc[:, :], ALU.add).then_inc(xbo, 1)

                for k in range(BLOCKS + 2):
                    if k < BLOCKS:
                        if k >= 3:
                            pool.wait_ge(o_norm, b * BLOCKS + k - 2)
                        pool.wait_ge(rinv_done, b * BLOCKS + k + 1)
                        if k >= 2:
                            pool.wait_ge(pv_done, b * BLOCKS + k - 1)
                        pool.sem_inc(pool_passed, 1)
                        for j in range(2):
                            last_bc = nc.gpsimd.tensor_scalar(rinv_bc[:, k % 2, j, :], ones[:, :],
                                                              rinv[:, 2 * k + j:2 * k + j + 1], None, ALU.mult)
                        last_bc.then_inc(rbc_done, 1)
                    if k >= 2:
                        m = k - 2
                        pair, odd, q = m // NT, m // QB % 2, m % QB
                        rows = slice(D * odd, D * odd + D)
                        if k < BLOCKS:
                            pool.wait_ge(rbc_done, b * BLOCKS + k + 1)
                        elif k == BLOCKS:
                            pool.wait_ge(xbo, b * NT + 4)
                        else:
                            pool.wait_ge(os_lo, b * PIECES + PIECES - 1)
                        pool.wait_ge(o_copied, b * BLOCKS + m + 1)
                        nc.gpsimd.tensor_tensor(oH[rows, m % 2, :], oH[rows, m % 2, :], oL[rows, m % 2, :],
                                                ALU.add).then_inc(o_sum, 1)
                        pool.wait_ge(o_sum, b * BLOCKS + m + 1)
                        nc.gpsimd.tensor_tensor(oT[rows, pair, q * QC:(q + 1) * QC], oH[rows, m % 2, :],
                                                Rs[rows, m % 2, :], ALU.mult).then_inc(o_norm, 1)
                        for j in range(EARLY):
                            if EARLY_BLOCK[j] == k:
                                low_of_output(j, m + 1)
                        if m >= BLOCKS - QB:
                            low_of_output(EARLY + m - (BLOCKS - QB), m + 1)
                        if BLOCKS - 2 <= k < BLOCKS:
                            for i in range(2):
                                add_bo(2 * (k - BLOCKS + 2) + i)
                for i in range(4, NT):
                    add_bo(i)
                if not last:
                    low_of_v(b + 1)
                pool.wait_ge(n2_out, b * (16 * NT) + 16 * NT)
                pool.wait_ge(aff_out, b * 16 + 16)
                pool.sem_inc(pool_passed, 1)

            all_images(pool, image)

        @block.scalar
        def _(act):
            def root(n, count, tiles):
                act.wait_ge(ve_done[n], count + 1)
                nc.scalar.activation(std[:, n, tiles], ve[:, n, tiles], ACT.Sqrt).then_inc(std_done[n], 1)

            def high_of_norm(j, i):
                k = ring_norm(i)
                act.wait_ge(ring_filled, j * RING + k + 1)
                nc.scalar.activation(nT[:, 0, :, i * P:(i + 1) * P],
                                     ring[:, k % 2, :].rearrange("p (k t) -> p k t", k=KC),
                                     ACT.Copy).then_inc(ring_hi, 1)

            def high_of_v(j, i):
                act.wait_ge(v_sum, j * NT + i + 1)
                src = tok[:, i % 4, :].rearrange("p (a h d) -> p a h d", a=PAIRS, h=2)
                nc.scalar.activation(V[:, i, :, 0:4:3, :], src, ACT.Copy).then_inc(v_hi, 1)

            def high_of_proj(j, p, r0=0, r1=4):
                for r in range(r0, r1):
                    k = ring_proj(p, r)
                    act.wait_ge(ring_filled, j * RING + k + 1)
                    cols = slice((r % 2) * 512, (r % 2) * 512 + 512)
                    for odd in range(2):
                        rows = slice(D * odd, D * odd + D)
                        dst = kd[rows, odd, 0, cols] if r < 2 else qs[rows, odd, cols]
                        nc.scalar.activation(dst, ring[rows, k % 2, :], ACT.Identity,
                                             bias=bqk[rows, 1 - r // 2, p:p + 1]).then_inc(ring_hi if odd else even_hi, 1)

            def exponentials(j, s):
                act.wait_ge(max_done, j * UNITS + s + 1)
                nc.scalar.activation(prob[:, s % 2, :], S[:, s % 2, :], ACT.Exp, bias=nmax[:, s:s + 1],
                                     accum_out=rsum[:, s:s + 1]).then_inc(exp_done, 1)

            def high_of_probs(j, u):
                for c in range(2):
                    k = ring_probs(u, c)
                    act.wait_ge(ring_filled, j * RING + k + 1)
                    if u // 2 >= 2 and u % 2 == 0 and c == 0:
                        act.wait_ge(pv_read, j * BLOCKS + u // 2 - 1)
                    nc.scalar.activation(PT[:, 0, u // 2 % 2, 4 * c:4 * c + 4, u % 2 * P:u % 2 * P + P],
                                         ring[:, k % 2, :].rearrange("p (m q) -> p m q", m=4),
                                         ACT.Copy).then_inc(ring_hi, 1)

            def high_of_weights(w):
                raw, hi, _, scale = splits[w]
                nc.scalar.activation(hi, raw, ACT.Copy, scale=scale).then_inc(w_hi, 1)

            act.wait_ge(ones_set, 1)
            nc.scalar.activation(unused[:, :], ones[:, 0:1], ACT.Sqrt)
            act.wait_ge(wv_raw_in, 16)
            high_of_weights(0)
            root(0, 0, slice(0, NT))
            act.wait_ge(wqk_raw_in, 32)
            for i in range(NT):
                high_of_norm(0, i)
                if i in (1, 3):
                    high_of_weights(1 + i // 2)
                if i >= 4:
                    high_of_v(0, i - 4)
            for i in range(4, NT):
                high_of_v(0, i)
            act.wait_ge(wo_raw_in, 16)
            high_of_weights(3)
            nc.scalar.activation(unused[:, :], ones[:, 0:1], ACT.Exp)
            act.wait_ge(bq_scaled, 1)
            act.wait_ge(w0_out, 16 * 4)
            act.wait_ge(w_out, 16 * 4 * (PAIRS - 1))
            high_of_proj(0, 0)
            act.wait_ge(wv_out, 16)
            act.wait_ge(v_lo, NT)
            exponentials(0, 0)
            exponentials(0, 1)
            high_of_probs(0, 0)

            def image(b, last):
                def high_of_output(j):
                    chunk, cols = piece(j)
                    act.wait_ge(o_norm, b * BLOCKS + blocks_of_piece(j))
                    nc.scalar.activation(oS[:, 0, chunk, cols], oT[:, chunk, cols], ACT.Copy).then_inc(os_hi, 1)

                def copy_output(m):
                    odd = m // QB % 2
                    rows, other = slice(D * odd, D * odd + D), slice(D * (1 - odd), D * (1 - odd) + D)
                    act.wait_ge(pv_done, b * BLOCKS + m + 1)
                    if m >= 2:
                        act.wait_ge(o_norm, b * BLOCKS + m - 1)
                    nc.scalar.activation(Rs[rows, m % 2, :], O[rows, m % 2, QC:2 * QC], ACT.Copy)
                    nc.scalar.activation(oH[rows, m % 2, :], O[rows, m % 2, 0:QC], ACT.Copy)
                    nc.scalar.activation(oL[rows, m % 2, :], O[other, m % 2, 0:QC], ACT.Copy).then_inc(o_copied, 1)

                for s in range(3, UNITS + 1):
                    act.wait_ge(ring_filled, b * RING + ring_probs(s - 3, 1) + 1)
                    exponentials(b, s - 1)
                    if s < UNITS and s % UP == 0:
                        high_of_proj(b, s // UP)
                    if s >= 8 and s % 2 == 0:
                        copy_output((s - 8) // 2)
                    high_of_probs(b, s - 2)
                    if s in EARLY_AT:
                        high_of_output(EARLY_AT.index(s))
                high_of_probs(b, UNITS - 1)
                high_of_output(EARLY)
                copy_output(BLOCKS - 3)
                if not last:
                    root(0, b + 1, slice(0, NT))
                copy_output(BLOCKS - 2)
                high_of_output(EARLY + 1)
                copy_output(BLOCKS - 1)
                high_of_output(EARLY + 2)
                high_of_output(EARLY + 3)
                for kind, i in WRAP:
                    if kind == "root":
                        root(1, b * 2 + i, slice(4 * i, 4 * i + 4))
                    if kind == "norm" and not last:
                        high_of_norm(b + 1, i)
                    if kind == "v" and not last:
                        high_of_v(b + 1, i)
                nc.scalar.activation(unused[:, :], ones[:, 0:1], ACT.Exp)
                if not last:
                    high_of_proj(b + 1, 0, 0, 3)

                def copy_logits(h):
                    act.wait_ge(logits, b * 2 + h + 1)
                    nc.scalar.activation(affT[:, 512 * h:512 * h + 512], O[0:E, h, :], ACT.Copy
                                         ).then_inc(logits_copied, 1)

                for i in range(NT):
                    if i == 2 and not last:
                        high_of_proj(b + 1, 0, 3, 4)
                    act.wait_ge(n2_filled, b * NT + i + 1)
                    nc.scalar.activation(n2T[:, i % 2, :, :], S4[:, 2 + i % 2, :].rearrange("p (k t) -> p k t", k=KC),
                                         ACT.Copy).then_inc(n2_copied, 1)
                    if i == 6:
                        copy_logits(0)
                if not last:
                    act.wait_ge(v_lo, b * NT + 2 * NT)
                    exponentials(b + 1, 0)
                copy_logits(1)
                act.wait_ge(soft, b * 5 + 2)
                nc.scalar.activation(lg[:, :, :], lg[:, :, :], ACT.Exp).then_inc(soft_exp, 1)
                if not last:
                    exponentials(b + 1, 1)
                    high_of_probs(b + 1, 0)
                for i in range(2):
                    act.wait_ge(affT_filled, b * 2 + i + 1)
                    nc.scalar.activation(affT[:, 512 * i:512 * i + 512], O[0:E, 1 - i, :], ACT.Copy
                                         ).then_inc(affT_copied, 1)

            all_images(act, image)

        @block.vector
        def _(dve):
            def low_of_weights(w):
                raw, hi, lo, scale = splits[w]
                dve.wait_ge(w_hi, w + 1)
                nc.vector.scalar_tensor_tensor(out=lo, in0=raw, scalar=scale, in1=hi.bitcast(F32),
                                               op0=ALU.mult, op1=ALU.subtract).then_inc(w_lo, 1)

            def statistics(n, j, i, src):
                nc.vector.bn_stats(stats[:, n, i, :], src).then_inc(stats_done[n], 1)

            def variance(n, count, tiles, done, eps):
                dve.wait_ge(stats_done[n], done)
                dve.sem_inc(dve_passed, 1)
                for i in range(tiles.start, tiles.stop):
                    last_mv = nc.vector.bn_aggr(mv[:, n, i, :], stats[:, n, i, :])
                last_mv.then_inc(mv_done[n], 1)
                dve.wait_ge(mv_done[n], count + 1)
                nc.vector.tensor_scalar(ve[:, n, tiles], mv[:, n, tiles, 1], eps, None, ALU.add
                                        ).then_inc(ve_done[n], 1)

            def inverse_root(n, count, tiles):
                a, c, out_r, v_e = r0[:, tiles], r1[:, tiles], rstd[:, n, tiles], ve[:, n, tiles]
                dve.wait_ge(std_done[n], count + 1)
                nc.vector.reciprocal(a, std[:, n, tiles]).then_inc(newton[n], 1)
                dve.wait_ge(newton[n], count * 5 + 1)
                nc.vector.tensor_tensor(c, a, a, ALU.mult).then_inc(newton[n], 1)
                dve.wait_ge(newton[n], count * 5 + 2)
                nc.vector.tensor_tensor(out_r, c, v_e, ALU.mult).then_inc(newton[n], 1)
                dve.wait_ge(newton[n], count * 5 + 3)
                nc.vector.tensor_scalar(c, out_r, -0.5, 1.5, ALU.mult, ALU.add).then_inc(newton[n], 1)
                dve.wait_ge(newton[n], count * 5 + 4)
                nc.vector.tensor_tensor(out_r, a, c, ALU.mult).then_inc(newton[n], 1)
                dve.wait_ge(newton[n], count * 5 + 5)

            def normalise(n, i, tile):
                nc.vector.tensor_scalar(tile, tile, mv[:, n, i, 0:1], rstd[:, n, i:i + 1],
                                        ALU.subtract, ALU.mult).then_inc(norm_done[n], 1)

            def low_of_norm(j, i):
                k = ring_norm(i)
                dve.wait_ge(ring_hi, j * RING + k + 1)
                nc.vector.tensor_tensor(nT[:, 1, :, i * P:(i + 1) * P],
                                        ring[:, k % 2, :].rearrange("p (k t) -> p k t", k=KC),
                                        nT[:, 0, :, i * P:(i + 1) * P].bitcast(F32),
                                        ALU.subtract).then_inc(ring_lo, 1)

            def sum_of_v(j, i):
                dve.wait_ge(v_filled, j * NT + i + 1)
                if i >= 4:
                    dve.wait_ge(v_lo, j * NT + i - 3)
                nc.vector.tensor_tensor(tok[:, i % 4, :], O[:, i % 2, :], bv_bc[:, :], ALU.add).then_inc(v_sum, 1)

            def low_of_proj(j, p, beside=None):
                for r in range(4):
                    if beside is not None:
                        beside(r)
                    k = ring_proj(p, r)
                    cols = slice((r % 2) * 512, (r % 2) * 512 + 512)
                    for odd in range(2):
                        if odd:
                            dve.wait_ge(ring_hi, j * RING + k + 1)
                        else:
                            dve.wait_ge(even_hi, j * (4 * PAIRS) + 4 * p + r + 1)
                        rows, other = slice(D * odd, D * odd + D), slice(D * (1 - odd), D * (1 - odd) + D)
                        hi, lo = ((kd[rows, odd, 0, cols], kd[rows, odd, 1, cols]) if r < 2 else
                                  (qs[rows, odd, cols], qs[other, odd, cols]))
                        last_lo = nc.vector.scalar_tensor_tensor(
                            out=lo, in0=ring[rows, k % 2, :], scalar=bqk[rows, 1 - r // 2, p:p + 1],
                            in1=hi.bitcast(F32), op0=ALU.add, op1=ALU.subtract)
                    last_lo.then_inc(ring_lo, 1)

            def maximum(j, s):
                dve.wait_ge(s_filled, j * UNITS + s + 1)
                nc.vector.tensor_reduce(nmax[:, s:s + 1], S[:, s % 2, :], AX.X, ALU.max, negate=True
                                        ).then_inc(max_done, 1)

            for i in range(NT):
                if i % 4 == 0:
                    dve.wait_ge(x_in[i // 4], 16)
                statistics(0, 0, i, xt[:, i, :])
            variance(0, 0, slice(0, NT), NT, EPS1)
            inverse_root(0, 0, slice(0, NT))
            dve.wait_ge(consts_in, 64)
            for i in range(NT + 2):
                if i < NT:
                    normalise(0, i, xt[:, i, :])
                if i in (3, 5, 7):
                    low_of_weights((i - 3) // 2)
                if i >= 2:
                    low_of_norm(0, i - 2)
                if i >= 6:
                    sum_of_v(0, i - 6)
            nc.vector.tensor_scalar(bqk[:, 0, :], bqk[:, 0, :], D ** -0.5, None, ALU.mult).then_inc(bq_scaled, 1)
            dve.wait_ge(bq_scaled, 1)
            for i in range(4, NT):
                sum_of_v(0, i)
            low_of_weights(3)
            low_of_proj(0, 0)
            maximum(0, 0)
            maximum(0, 1)

            def image(b, last):
                def tile_t(i):
                    dve.wait_ge(y_filled, b * NT + i + 1)
                    dve.wait_ge(xbo, b * NT + i + 1)
                    nc.vector.tensor_tensor(res(i), S4[:, i % 4, :], res(i), ALU.add).then_inc(t_done, 1)
                    dve.wait_ge(t_done, b * NT + i + 1)
                    statistics(1, b, i, res(i))

                for s in range(2, UNITS + 2):
                    if s < UNITS and s % UP == 0:
                        p = s // UP

                        def next_statistics(r):
                            i = 4 * (p - 1) + r
                            if r == 0:
                                dve.wait_ge(x_in[p - 1], b * 16 + 32)
                            statistics(0, b + 1, i, xt[:, i, :])

                        low_of_proj(b, p, next_statistics if p < 3 and not last else None)
                        if p == 2 and not last:
                            variance(0, b + 1, slice(0, NT), b * NT + 2 * NT, EPS1)
                    if s < UNITS and s % UP != 0:
                        maximum(b, s)
                    u = s - 2
                    for c in range(2):
                        k = ring_probs(u, c)
                        here = (u // 2 % 2, slice(4 * c, 4 * c + 4), slice(u % 2 * P, u % 2 * P + P))
                        dve.wait_ge(ring_hi, b * RING + k + 1)
                        nc.vector.tensor_tensor(PT[:, 1, here[0], here[1], here[2]],
                                                ring[:, k % 2, :].rearrange("p (m q) -> p m q", m=4),
                                                PT[:, 0, here[0], here[1], here[2]].bitcast(F32),
                                                ALU.subtract).then_inc(ring_lo, 1)
                        if c == 0 and s < UNITS and s % UP == 0:
                            maximum(b, s)
                    if u % 2 == 1:
                        dve.wait_ge(exp_done, b * UNITS + u + 1)
                        nc.vector.reciprocal(rinv[:, u - 1:u + 1], rsum[:, u - 1:u + 1]).then_inc(rinv_done, 1)
                if not last:
                    inverse_root(0, b + 1, slice(0, NT))
                for i in range(NT):
                    if i == 1:
                        tile_t(0)
                        tile_t(1)
                    if i == 2:
                        tile_t(2)
                        tile_t(3)
                        variance(1, b * 2, slice(0, 4), b * NT + 4, EPS2)
                    if not last:
                        normalise(0, i, xt[:, i, :])
                for kind, i in WRAP:
                    if kind == "root":
                        inverse_root(1, b * 2 + i, slice(4 * i, 4 * i + 4))
                    if kind == "t":
                        tile_t(i)
                        if i == NT - 1:
                            variance(1, b * 2 + 1, slice(4, 8), b * NT + NT, EPS2)
                    if kind == "n2":
                        if i % 4 == 0:
                            dve.wait_ge(t_out[i // 4], b * 64 + 64)
                        normalise(1, i, res(i))
                    if kind == "norm" and not last:
                        low_of_norm(b + 1, i)
                    if kind == "v" and not last:
                        sum_of_v(b + 1, i)
                if not last:
                    low_of_proj(b + 1, 0)
                    maximum(b + 1, 0)
                    maximum(b + 1, 1)
                dve.wait_ge(logits_turned, b + 1)
                lgp = O[:, 0, 0:NT * E].rearrange("p (i e) -> p i e", e=E)
                nc.vector.tensor_reduce(gmax[:, :], lgp, AX.X, ALU.max).then_inc(soft, 1)
                dve.wait_ge(soft, b * 5 + 1)
                nc.vector.tensor_tensor(lg[:, :, :], lgp, gmax[:, :].unsqueeze(2).broadcast_to([P, NT, E]),
                                        ALU.subtract).then_inc(soft, 1)
                dve.wait_ge(soft_exp, b + 1)
                nc.vector.tensor_reduce(gsum[:, :], lg[:, :, :], AX.X, ALU.add).then_inc(soft, 1)
                dve.wait_ge(soft, b * 5 + 3)
                nc.vector.reciprocal(grec[:, :], gsum[:, :]).then_inc(soft, 1)
                dve.wait_ge(soft, b * 5 + 4)
                nc.vector.tensor_tensor(aff[:, :, :], lg[:, :, :], grec[:, :].unsqueeze(2).broadcast_to([P, NT, E]),
                                        ALU.mult).then_inc(soft, 1)

            all_images(dve, image)

        @block.tensor
        def _(pe):
            def products(dst, pairs):
                for n, (l, r) in enumerate(pairs):
                    last_mm = nc.tensor.matmul(dst, l, r, start=(n == 0), stop=(n == len(pairs) - 1))
                return last_mm

            HL = [(0, 0), (0, 1), (1, 0)]

            def turn_norm(j, i, first):
                k = ring_norm(i)
                pe.wait_ge(norm_done[0], j * NT + i + 1)
                if not first or i >= 2:
                    pe.wait_ge(ring_lo, j * RING + k - 1)
                for c in range(KC):
                    last_t = nc.tensor.transpose(ring[:, k % 2, c * P:(c + 1) * P], xt[:, i, c * P:(c + 1) * P], ident)
                last_t.then_inc(ring_filled, 1)

            def project_v(j, i):
                pe.wait_ge(ring_lo, j * RING + ring_norm(i) + 1)
                if i >= 2:
                    pe.wait_ge(v_sum, j * NT + i - 1)
                products(O[:, i % 2, :], [(nT[:, l, c, i * P:(i + 1) * P], wv[:, w, c, :])
                                          for c in range(KC) for l, w in HL]).then_inc(v_filled, 1)

            def project_pair(j, p, r0=0, r1=4):
                w = wqk if p else w0
                if r0 == 0:
                    if p:
                        pe.wait_ge(wqk_in, j * (16 * (PAIRS - 1)) + 16 * p)
                    else:
                        pe.wait_ge(w0_in, j * 16 + 16)
                for r in range(r0, r1):
                    k = ring_proj(p, r)
                    pe.wait_ge(ring_lo, j * RING + k - 1)
                    products(ring[:, k % 2, :],
                             [(w[:, 2 * (1 - r // 2) + h, c, :], nT[:, l, c, (r % 2) * 512:(r % 2) * 512 + 512])
                              for c in range(KC) for h, l in HL]).then_inc(ring_filled, 1)

            def scores(j, s):
                odd, i = s // NT % 2, s % NT
                if s % UP == 0:
                    pe.wait_ge(ring_lo, j * RING + ring_proj(s // UP, 3) + 1)
                    pe.wait_ge(k_dup, j * (64 * PAIRS) + 64 * (s // UP) + 64)
                if s >= 2:
                    pe.wait_ge(exp_done, j * UNITS + s - 1)
                for m in range(2):
                    for l in range(2):
                        last_mm = nc.tensor.matmul(S[:, s % 2, 512 * m:512 * m + 512], qs[:, odd, i * P:(i + 1) * P],
                                                   kd[:, odd, l, 512 * m:512 * m + 512],
                                                   start=(l == 0), stop=(l == 1))
                last_mm.then_inc(s_filled, 1)

            def turn_probs(j, u, c):
                k = ring_probs(u, c)
                pe.wait_ge(exp_done, j * UNITS + u + 1)
                pe.wait_ge(ring_lo, j * RING + k - 1)
                for m in range(4):
                    last_t = nc.tensor.transpose(ring[:, k % 2, m * P:(m + 1) * P],
                                                 prob[:, u % 2, (4 * c + m) * P:(4 * c + m + 1) * P], ident)
                last_t.then_inc(ring_filled, 1)

            for i in range(NT):
                turn_norm(0, i, True)
                if i == 3:
                    pe.wait_ge(w_lo, 1)
                if i >= 3:
                    project_v(0, i - 3)
            for i in range(NT - 3, NT):
                project_v(0, i)
            project_pair(0, 0)
            scores(0, 0)
            scores(0, 1)
            turn_probs(0, 0, 0)
            turn_probs(0, 0, 1)
            scores(0, 2)
            pe.wait_ge(w_lo, 4)

            def image(b, last):
                def product_with_v(m, part):
                    head = m // QB
                    if part == 0:
                        if m == 0:
                            pe.wait_ge(v_lo, b * NT + NT)
                        if m >= 2:
                            pe.wait_ge(o_copied, b * BLOCKS + m - 1)
                        pe.wait_ge(ring_lo, b * RING + ring_probs(2 * m + 1, 1) + 1)
                    for t in range(2 * part, 2 * part + 2):
                        for l in range(2):
                            last_mm = nc.tensor.matmul(
                                O[:, m % 2, 0:QC],
                                V[:, t, head // 2, 2 * (head % 2):2 * (head % 2) + 2, :].rearrange("p h d -> p (h d)"),
                                PT[:, l, m % 2, t, :],
                                start=(t + l == 0), stop=(t == NT - 1 and l == 1))
                    if part == 3:
                        last_mm.then_inc(pv_read, 1)

                def inverse_sums(m):
                    pe.wait_ge(rbc_done, b * BLOCKS + m + 1)
                    for j in range(2):
                        last_t = nc.tensor.transpose(O[:, m % 2, QC + j * P:QC + (j + 1) * P],
                                                     rinv_bc[:, m % 2, j, :], ident)
                    last_t.then_inc(pv_done, 1)

                def turn_and_multiply(u, m, half):
                    for c in range(2):
                        if m >= 0:
                            product_with_v(m, 2 * half + c)
                        turn_probs(b, u, c)
                    if m >= 0 and half == 1:
                        inverse_sums(m)

                def project_out(i, part):
                    if part == 0:
                        pe.wait_ge(os_lo, b * PIECES + EARLY)
                        if i < 4:
                            pe.wait_ge(exp_done, b * UNITS + UNITS - 1 + i // 2)
                        else:
                            pe.wait_ge(t_done, b * NT + i - 3)
                    else:
                        pe.wait_ge(os_lo, b * PIECES + EARLY + i // 2 + 1)
                    for c in range(KC - 1) if part == 0 else [KC - 1]:
                        for n, (l, w) in enumerate(HL):
                            last_mm = nc.tensor.matmul(S4[:, i % 4, :], oS[:, l, c, i * P:(i + 1) * P], wo[:, w, c, :],
                                                       start=(c + n == 0), stop=(c == KC - 1 and n == 2))
                    if part == 1:
                        last_mm.then_inc(y_filled, 1)

                for s in range(3, UNITS):
                    m, half = (s - 5) // 2, (s - 5) % 2
                    if s % UP == 0:
                        product_with_v(m, 0)
                        product_with_v(m, 1)
                        project_pair(b, s // UP)
                        turn_probs(b, s - 2, 0)
                        product_with_v(m, 2)
                        product_with_v(m, 3)
                        inverse_sums(m)
                        turn_probs(b, s - 2, 1)
                        scores(b, s)
                    else:
                        scores(b, s)
                        turn_and_multiply(s - 2, -1 if s % UP == UP - 1 and s < UNITS - 1 else m, half)
                turn_and_multiply(UNITS - 2, BLOCKS - 3, 1)
                project_out(0, 0)
                turn_and_multiply(UNITS - 1, BLOCKS - 2, 0)
                project_out(1, 0)
                product_with_v(BLOCKS - 2, 2)
                product_with_v(BLOCKS - 2, 3)
                inverse_sums(BLOCKS - 2)
                project_out(2, 0)
                for part in range(4):
                    product_with_v(BLOCKS - 1, part)
                inverse_sums(BLOCKS - 1)
                project_out(0, 1)
                project_out(1, 1)
                project_out(3, 0)
                project_out(2, 1)
                project_out(3, 1)
                for kind, i in WRAP:
                    if kind == "t":
                        project_out(i, 0)
                        project_out(i, 1)
                    if kind == "norm" and not last:
                        turn_norm(b + 1, i, False)
                    if kind == "v" and not last:
                        if i == 0:
                            pe.wait_ge(wv_in, b * 16 + 16)
                            pe.wait_ge(o_copied, b * BLOCKS + BLOCKS)
                        project_v(b + 1, i)
                def turn_n2(i):
                    pe.wait_ge(norm_done[1], b * NT + i + 1)
                    if i >= 2:
                        pe.wait_ge(n2_copied, b * NT + i - 1)
                    for c in range(KC):
                        last_t = nc.tensor.transpose(S4[:, 2 + i % 2, c * P:(c + 1) * P],
                                                     res(i)[:, c * P:(c + 1) * P], ident)
                    last_t.then_inc(n2_filled, 1)

                if not last:
                    project_pair(b + 1, 0, 0, 3)
                pe.wait_ge(t_done, b * NT + NT)
                turn_n2(0)
                turn_n2(1)
                if last:
                    pe.wait_ge(o_copied, b * BLOCKS + BLOCKS)
                else:
                    project_pair(b + 1, 0, 3, 4)
                    pe.wait_ge(v_sum, b * NT + 2 * NT)
                for i in range(NT):
                    pe.wait_ge(n2_copied, b * NT + i + 1)
                    last_mm = products(O[0:E, i // 4, i % 4 * P:i % 4 * P + P],
                                       [(gate_sb[:, c, :], n2T[:, i % 2, c, :]) for c in range(KC)])
                    if i % 4 == 3:
                        last_mm.then_inc(logits, 1)
                    if i < NT - 2:
                        turn_n2(i + 2)
                    if i == NT - 3 and not last:
                        scores(b + 1, 0)
                if not last:
                    scores(b + 1, 1)
                pe.wait_ge(logits_copied, b * 2 + 2)
                pe.sem_inc(pe_passed, 1)
                for i in range(NT):
                    last_t = nc.tensor.transpose(O[:, 0, i * E:(i + 1) * E], affT[:, i * P:(i + 1) * P],
                                                 ident[0:E, 0:E])
                last_t.then_inc(logits_turned, 1)
                if not last:
                    turn_probs(b + 1, 0, 0)
                    turn_probs(b + 1, 0, 1)
                    scores(b + 1, 2)
                pe.wait_ge(soft, b * 5 + 5)
                for h in range(2):
                    for i in range(4):
                        last_t = nc.tensor.transpose(O[0:E, 1 - h, i * P:(i + 1) * P], aff[:, 4 * h + i, :], ident)
                    last_t.then_inc(affT_filled, 1)

            all_images(pe, image)


def program(nc, out, x, wT, b_row, b_col, gate, w1, w2, b1, b2):
    n2 = nc.dram_tensor("n2_rows", [B, N, C], F32).ap()
    aff = nc.dram_tensor("affinities", [B, E, N], F32).ap()
    with ExitStack() as ctx:
        ident = ctx.enter_context(nc.sbuf_tensor("ident", [P, P], F32))
        idx = ctx.enter_context(nc.sbuf_tensor("idx", [P, E * B], U32))
        gates = ctx.enter_context(nc.sbuf_tensor("gates", [P, E * B], F32))
        ident_made = ctx.enter_context(nc.semaphore("ident_made"))
        with nc.Block() as block:
            @block.gpsimd
            def _(pool):
                nc.gpsimd.memset(ident[:, :], 0.0).then_inc(ident_made, 1)
                pool.wait_ge(ident_made, 1)
                nc.gpsimd.affine_select(out=ident[:, :], in_=ident[:, :], compare_op=ALU.not_equal, fill=1.0,
                                        base=0, pattern=[[-1, P]], channel_multiplier=1).then_inc(ident_made, 1)
                pool.wait_ge(ident_made, 2)
        attention(nc, x, wT, b_row, b_col, gate, out, n2, aff, ident[:, :])
        experts(nc, aff, w1, w2, b1, b2, out.rearrange("b n c -> (b n) c"), n2.rearrange("b n c -> (b n) c"),
                ident[:, :], idx[:, :], gates[:, :])


def experts(nc, aff_dram, w1, w2, b1, b2, out_rows, n2_rows, ident, idx, gates):
    STEPS = CAP // 8
    G = 4
    COLS = G * CAP
    with ExitStack() as ctx:
        def sb(name, shape, dt=F32):
            return ctx.enter_context(nc.sbuf_tensor(name, shape, dt))

        def sem(name):
            return ctx.enter_context(nc.semaphore(name))

        wraw = sb("wraw", [P, 2 * KC, FF])
        ws = sb("ws", [P, 2, 2, 2 * KC, FF], F32R)
        b1s = sb("b1s", [P, 2, KC])
        b2s = sb("b2s", [P, 2, C])
        idxc = sb("idxc", [P, 2, B], U32)
        gatec = sb("gatec", [P, 2, B])
        xg = sb("xg", [P, 2, G, C])
        xT = sb("xT", [P, 2, 2, KC, COLS], F32R)
        hf = sb("hf", [P, 2, COLS])
        hT = sb("hT", [P, 2, KC, COLS], F32R)
        y0 = sb("y0", [P, 2, C])
        y = sb("y", [P, 2, G, C])
        work = sb("work", [P, 2, N])
        top8 = sb("top8", [P, CAP])
        pos = sb("pos", [P, CAP], U32)
        posf = sb("posf", [P, CAP])
        base_i = sb("base_i", [P, B, E], mybir.dt.int32)
        base_f = sb("base_f", [P, B, E])
        xr = ctx.enter_context(nc.psum_tensor("xr", [P, 2, 512], F32))
        p1 = ctx.enter_context(nc.psum_tensor("p1", [P, 2, 512], F32))
        p2 = ctx.enter_context(nc.psum_tensor("p2", [P, 4, 512], F32))

        aff_in = sem("aff_in")
        base_made = sem("base_made")
        picked = sem("picked")
        rows_made = sem("rows_made")
        turned = sem("turned")
        chosen = sem("chosen")
        w_in = sem("w_in")
        b12_in = [sem(f"b12_in{i}") for i in range(2)]
        ws_hi = sem("ws_hi")
        ws_lo = sem("ws_lo")
        cols_made = sem("cols_made")
        gathered = [sem(f"gathered{i}") for i in range(2)]
        xr_filled = sem("xr_filled")
        xr_hi = sem("xr_hi")
        xr_lo = sem("xr_lo")
        p1_filled = sem("p1_filled")
        h_done = sem("h_done")
        h_hi = sem("h_hi")
        h_lo = sem("h_lo")
        p2_filled = sem("p2_filled")
        y0_done = sem("y0_done")
        y_done = sem("y_done")
        added = [sem(f"added{i}") for i in range(B)]
        sp_passed2, pool_passed2 = sem("sp_passed2"), sem("pool_passed2")
        block = ctx.enter_context(nc.Block())
        WCH = 2 * KC

        def every_expert(engine, expert):
            expert(0, 0, False)
            expert(1, 1, False)
            with engine.Fori(1, E // 2 - 1) as twos:
                expert(2 * twos, 0, False)
                expert(2 * twos + 1, 1, False)
            expert(E - 2, 0, False)
            expert(E - 1, 1, True)

        def started(e, g, n):
            return type(e) is not int or e > 0 or g > 0 or n >= 0

        @block.sync
        def _(sp):
            def load(e, k):
                sp.dma_start(wraw[:, 0:KC, :], w1[e]).then_inc(w_in, 16)
                sp.dma_start(wraw[:, KC:2 * KC, :], w2[e]).then_inc(w_in, 16)
                sp.dma_start(b1s[:, k, :], b1[e]).then_inc(b12_in[k], 16)
                sp.dma_start(b2s[:, k, :], b2[e].broadcast_to([P, C])).then_inc(b12_in[k], 16)

            sp.dma_start(work[:, 0, :], aff_dram.rearrange("b e n -> (b e) n")).then_inc(aff_in, 16)
            load(0, 0)
            sp.wait_ge(ws_lo, WCH)
            load(1, 1)
            with sp.Fori(0, E // 2 - 1) as twos:
                for k in range(2):
                    e = 2 * twos
                    sp.wait_ge(ws_lo, (e + k) * WCH + 2 * WCH)
                    sp.sem_inc(sp_passed2, 1)
                    sp.wait_ge(y0_done, (e + k) * (2 * G) + 2 * G)
                    load(e + k + 2, k)

        @block.gpsimd
        def _(pool):
            def columns(e, k):
                nc.gpsimd.tensor_copy(idxc[:, k, :], idx[:, bass.ds(e * B, B)])
                nc.gpsimd.tensor_copy(gatec[:, k, :], gates[:, bass.ds(e * B, B)]).then_inc(cols_made, 1)

            def gather(k, g):
                for j in range(G):
                    pool.indirect_dma_start(
                        out=xg[:, g, j, :], out_offset=None, in_=n2_rows,
                        in_offset=bass.IndirectOffsetOnAxis(ap=idxc[:, k, G * g + j:G * g + j + 1], axis=0),
                    ).then_inc(gathered[g], 16)

            def scatter(e, k, g):
                for j in range(G):
                    pool.wait_ge(y_done, e * (2 * G) + G * g + j + 1)
                    if type(e) is not int or e > 0:
                        pool.wait_ge(added[G * g + j], e * 16)
                    pool.sem_inc(pool_passed2, 1)
                    pool.indirect_dma_start(
                        out=out_rows, out_offset=bass.IndirectOffsetOnAxis(ap=idxc[:, k, G * g + j:G * g + j + 1], axis=0),
                        in_=y[:, g, j, :], in_offset=None, compute_op=ALU.add,
                    ).then_inc(added[G * g + j], 16)

            def expert(e, k, last):
                if not last:
                    if type(e) is not int or e > 0:
                        pool.wait_ge(y_done, e * (2 * G))
                        for i in range(B):
                            pool.wait_ge(added[i], e * 16)
                    columns(e + 1, 1 - k)
                    pool.wait_ge(cols_made, e + 2)
                for g in range(2):
                    if not last:
                        pool.wait_ge(xr_filled, e * (2 * G) + G * g + G)
                        pool.sem_inc(pool_passed2, 1)
                        gather(1 - k, g)
                    scatter(e, k, g)

            nc.gpsimd.iota(base_i[:, :, :], pattern=[[N, B], [0, E]], base=0, channel_multiplier=0
                           ).then_inc(base_made, 1)
            for c in range(WCH):
                pool.wait_ge(ws_hi, c + 1)
                nc.gpsimd.tensor_tensor(ws[:, 0, 1, c, :], wraw[:, c, :], ws[:, 0, 0, c, :].bitcast(F32),
                                        ALU.subtract).then_inc(ws_lo, 1)
            pool.wait_ge(chosen, 2)
            columns(0, 0)
            pool.wait_ge(cols_made, 1)
            gather(0, 0)
            gather(0, 1)
            every_expert(pool, expert)
            for i in range(B):
                pool.wait_ge(added[i], 16 * E)

        @block.scalar
        def _(act):
            def turn(v, g, j):
                act.wait_ge(xr_filled, v * G + j + 1)
                nc.scalar.activation(xT[:, g, 0, :, j * P:(j + 1) * P],
                                     xr[:, j % 2, :].rearrange("p (k t) -> p k t", k=KC),
                                     ACT.Copy).then_inc(xr_hi, 1)

            def expert(e, k, last):
                act.wait_ge(b12_in[k], (e - k) * 16 + 32)
                act.wait_ge(cols_made, e + 1)
                for g in range(2):
                    v = e * 2 + g
                    for m in range(KC):
                        act.wait_ge(p1_filled, v * KC + m + 1)
                        if started(e, g, m - 2):
                            act.wait_ge(h_lo, v * KC + m - 1)
                        nc.scalar.activation(hf[:, m % 2, :], p1[:, m % 2, :], ACT.Gelu_apprx_tanh,
                                             bias=b1s[:, k, m:m + 1]).then_inc(h_done, 1)
                    more = not (last and g == 1)
                    for j in range(2):
                        if more:
                            turn(v + 1, 1 - g, j)
                    for j in range(G):
                        if more and j < 2:
                            turn(v + 1, 1 - g, 2 + j)
                        act.wait_ge(y0_done, v * G + j + 1)
                        if started(e, 0, -1):
                            act.wait_ge(added[G * g + j], e * 16)
                        nc.scalar.activation(y[:, g, j, :], y0[:, j % 2, :], ACT.Copy,
                                             scale=gatec[:, k, G * g + j:G * g + j + 1]).then_inc(y_done, 1)

            act.wait_ge(w_in, 32)
            for c in range(WCH):
                nc.scalar.activation(ws[:, 0, 0, c, :], wraw[:, c, :], ACT.Copy).then_inc(ws_hi, 1)
            for j in range(G):
                turn(0, 0, j)
            every_expert(act, expert)

        @block.vector
        def _(dve):
            def split_chunk(e, k, c):
                if c == 0:
                    dve.wait_ge(w_in, e * 32 + 32)
                nc.vector.tensor_copy(ws[:, k, 0, c, :], wraw[:, c, :]).then_inc(ws_hi, 1)
                dve.wait_ge(ws_hi, e * WCH + c + 1)
                nc.vector.tensor_tensor(ws[:, k, 1, c, :], wraw[:, c, :], ws[:, k, 0, c, :].bitcast(F32),
                                        ALU.subtract).then_inc(ws_lo, 1)

            def turn(v, g, j):
                dve.wait_ge(xr_hi, v * G + j + 1)
                nc.vector.tensor_tensor(xT[:, g, 1, :, j * P:(j + 1) * P],
                                        xr[:, j % 2, :].rearrange("p (k t) -> p k t", k=KC),
                                        xT[:, g, 0, :, j * P:(j + 1) * P].bitcast(F32),
                                        ALU.subtract).then_inc(xr_lo, 1)

            def expert(e, k, last):
                dve.wait_ge(b12_in[k], (e - k) * 16 + 32)
                for g in range(2):
                    v = e * 2 + g
                    for m in range(KC):
                        dve.wait_ge(h_done, v * KC + m + 1)
                        if m == 0 and started(e, g, -1):
                            dve.wait_ge(p2_filled, v * G)
                        nc.vector.tensor_copy(hT[:, 0, m, :], hf[:, m % 2, :]).then_inc(h_hi, 1)
                        dve.wait_ge(h_hi, v * KC + m + 1)
                        nc.vector.tensor_tensor(hT[:, 1, m, :], hf[:, m % 2, :], hT[:, 0, m, :].bitcast(F32),
                                                ALU.subtract).then_inc(h_lo, 1)
                        if not last and g == 0 and m >= 2:
                            split_chunk(e + 1, 1 - k, m - 2)
                        if not last and g == 1 and m < 3:
                            split_chunk(e + 1, 1 - k, KC + m)
                    more = not (last and g == 1)
                    for j in range(2):
                        if more:
                            turn(v + 1, 1 - g, j)
                    for j in range(G):
                        if more and j in (1, 2):
                            turn(v + 1, 1 - g, 1 + j)
                        dve.wait_ge(p2_filled, v * G + j + 1)
                        if started(e, g, j - 2):
                            dve.wait_ge(y_done, v * G + j - 1)
                        nc.vector.tensor_tensor(y0[:, j % 2, :], p2[:, j, :], b2s[:, k, :], ALU.add
                                                ).then_inc(y0_done, 1)
                        if not last and g == 0 and j >= 2:
                            split_chunk(e + 1, 1 - k, j)
                        if not last and g == 1 and j == 2:
                            split_chunk(e + 1, 1 - k, 2 * KC - 1)

            dve.wait_ge(aff_in, 16)
            for r in range(STEPS):
                src, dst = work[:, r % 2, :], work[:, 1 - r % 2, :]
                best = top8[:, 8 * r:8 * r + 8]
                nc.vector.max(best, src).then_inc(picked, 1)
                dve.wait_ge(picked, 2 * r + 1)
                nc.vector.max_index(pos[:, 8 * r:8 * r + 8], best, src)
                nc.vector.match_replace(dst, best, src, -1.0).then_inc(picked, 1)
                dve.wait_ge(picked, 2 * r + 2)
            nc.vector.tensor_copy(posf[:, :], pos[:, :]).then_inc(rows_made, 1)
            dve.wait_ge(base_made, 1)
            nc.vector.tensor_copy(base_f[:, :, :], base_i[:, :, :]).then_inc(rows_made, 1)
            dve.wait_ge(rows_made, 2)
            dve.wait_ge(turned, 1)
            nc.vector.tensor_tensor(idx.rearrange("p (e b) -> p b e", e=E),
                                    p2[:, 0, 0:P].rearrange("p (b e) -> p b e", e=E), base_f[:, :, :],
                                    ALU.add).then_inc(chosen, 1)
            dve.wait_ge(turned, 2)
            nc.vector.tensor_copy(gates.rearrange("p (e b) -> p b e", e=E),
                                  p2[:, 1, 0:P].rearrange("p (b e) -> p b e", e=E)).then_inc(chosen, 1)
            for j in range(G):
                turn(0, 0, j)
            every_expert(dve, expert)

        @block.tensor
        def _(pe):
            HL = [(0, 0), (0, 1), (1, 0)]

            def products(dst, pairs):
                for n, (l, r) in enumerate(pairs):
                    last = nc.tensor.matmul(dst, l, r, start=(n == 0), stop=(n == len(pairs) - 1))
                return last

            def turn(e, v, g, j):
                if j == 0:
                    pe.wait_ge(gathered[g], e * (16 * G) + 16 * G)
                if type(v) is not int or v > 0 or j >= 2:
                    pe.wait_ge(xr_lo, v * G + j - 1)
                for c in range(KC):
                    last = nc.tensor.transpose(xr[:, j % 2, c * P:(c + 1) * P], xg[:, g, j, c * P:(c + 1) * P],
                                               ident)
                last.then_inc(xr_filled, 1)

            def expert(e, k, last):
                pe.wait_ge(ws_lo, e * WCH + WCH)
                for g in range(2):
                    v = e * 2 + g
                    pe.wait_ge(xr_lo, v * G + G)
                    for m in range(KC):
                        if started(e, g, m - 2):
                            pe.wait_ge(h_done, v * KC + m - 1)
                        products(p1[:, m % 2, :], [(ws[:, k, w, c, m * P:(m + 1) * P], xT[:, g, l, c, :])
                                                   for c in range(KC) for w, l in HL]).then_inc(p1_filled, 1)
                    more = not (last and g == 1)
                    for j in range(2):
                        if more:
                            turn(e + g, v + 1, 1 - g, j)
                    for j in range(G):
                        if more and j in (1, 2):
                            turn(e + g, v + 1, 1 - g, 1 + j)
                        if started(e, g, -1):
                            pe.wait_ge(y0_done, v * G + j - 3)
                        for c in range(KC):
                            if j == 0:
                                pe.wait_ge(h_lo, v * KC + c + 1)
                            for n, (l, w) in enumerate(HL):
                                prod = nc.tensor.matmul(p2[:, j, :], hT[:, l, c, j * P:(j + 1) * P],
                                                        ws[:, k, w, KC + c, :],
                                                        start=(c + n == 0), stop=(c == KC - 1 and n == 2))
                        prod.then_inc(p2_filled, 1)

            pe.wait_ge(rows_made, 1)
            nc.tensor.transpose(p2[:, 0, 0:P], posf[:, :], ident).then_inc(turned, 1)
            nc.tensor.transpose(p2[:, 1, 0:P], top8[:, :], ident).then_inc(turned, 1)
            for j in range(G):
                turn(0, 0, 0, j)
            every_expert(pe, expert)


_OUT = "out_dram"


def kernel(**inputs):
    import numpy as np
    import concourse.bacc as bacc
    from concourse.bass_utils import run_bass_kernel_spmd

    nc = bacc.Bacc("TRN2", target_bir_lowering=False, num_devices=1)
    a = {k: np.asarray(v) for k, v in inputs.items()}

    def chunks(w):
        return w.reshape(*w.shape[:-2], KC, P, w.shape[-1]).swapaxes(-3, -2)

    biases = [a["L0_conv_bq"], a["L0_conv_bk"], a["L0_conv_bv"], a["L0_conv_bo"]]
    arrays = {
        "x_dram": a["x"].reshape(B, C, N).transpose(0, 2, 1),
        "wT_dram": np.stack([chunks(a["L0_conv_" + n].T) for n in ("Wq", "Wk", "Wv", "Wo")]),
        "b_row_dram": np.stack(biases),
        "b_col_dram": np.stack([v.reshape(KC, P).T for v in biases[:2]], 1),
        "gate_dram": chunks(a["L0_ffn_gate_weight"]),
        "w1_dram": chunks(a["L0_ffn_w1"]),
        "w2_dram": chunks(a["L0_ffn_w2"]),
        "b1_dram": a["L0_ffn_b1"].reshape(E, KC, P).transpose(0, 2, 1),
        "b2_dram": a["L0_ffn_b2"].reshape(E, 1, C),
    }
    arrays = {k: np.ascontiguousarray(v) for k, v in arrays.items()}
    d = {k: nc.dram_tensor(k, v.shape, F32, kind="ExternalInput").ap() for k, v in arrays.items()}
    out = nc.dram_tensor(_OUT, (B, N, C), F32, kind="ExternalOutput").ap()
    program(nc, out, **{k.removesuffix("_dram"): v for k, v in d.items()})
    r = run_bass_kernel_spmd(nc, [arrays], core_ids=[0])
    return np.ascontiguousarray(r.results[0][_OUT].transpose(0, 2, 1)).reshape(B, C, 32, 32)
```
